# Optimizing a Trainium2 kernel written in Bass

```python
import numpy as np
import jax
import jax.numpy as jnp

def _softmax(x, axis=-1):
    return jax.nn.softmax(x, axis=axis)

def _gelu(x):
    return jax.nn.gelu(x, approximate=True)

def _silu(x):
    return jax.nn.silu(x)

def _sigmoid(x):
    return jax.nn.sigmoid(x)

def _layernorm(x, axis=-1, eps=1e-05):
    m = jnp.mean(x, axis=axis, keepdims=True)
    v = jnp.var(x, axis=axis, keepdims=True)
    return (x - m) / jnp.sqrt(v + eps)

def _scatter_add(tgt, idx, src, axis=0):
    return tgt.at[idx].add(src)

def _segment_sum(src, seg, n):
    return jax.ops.segment_sum(src, seg, n)
kernel_name = 'mk_xattn_ffn_d2_seqx_r8_17aa67'

def setup_inputs(seed: int=0):
    np.random.seed(seed)
    _w = jnp.asarray

    def _rec_inputs():
        import jax
        import jax.numpy as jnp
        _rk = jax.random.key(seed)
        x = -0.0002928 + 1 * jax.random.normal(jax.random.fold_in(_rk, 1), (128, 64, 128), jnp.float32)
        _lenS = 64 - jax.random.randint(jax.random.fold_in(_rk, 7), (128,), 0, max(1, 64 // 4) + 1, jnp.int32)
        _lenS2 = 64 - jax.random.randint(jax.random.fold_in(_rk, 8), (128,), 0, max(1, 64 // 4) + 1, jnp.int32)
        _ctx_1024P = jax.random.normal(jax.random.fold_in(_rk, 11), (128, 16, 128), jnp.float32)
        _ctx_1024c = jax.random.dirichlet(jax.random.fold_in(_rk, 511), 0.3 * jnp.ones((16,), jnp.float32), (128, 64))
        _ctx_1024t = jnp.einsum('bsk,bkd->bsd', _ctx_1024c, _ctx_1024P)
        _ctx_1024t = _ctx_1024t * jax.lax.rsqrt(jnp.mean(jnp.square(_ctx_1024t)) + 1e-12) * 0.953939
        ctx_1024 = -1.39393e-06 + 0.999914 * (_ctx_1024t + 0.3 * jax.random.normal(jax.random.fold_in(_rk, 611), (128, 64, 128), jnp.float32))
        return (x, ctx_1024)
    x, ctx_1024 = _rec_inputs()

    def _L0_xattn_setup():
        import jax, jax.numpy as jnp
        import numpy as np
        H = 16
        key = jax.random.key(seed)
        ks = jax.random.split(key, 11)
        B, S, D = (2, 256, 128)
        sc = 0.02
        return {'q_in': jax.random.normal(ks[0], (B, S, D), jnp.float32), 'k_in': jax.random.normal(ks[1], (B, S, D), jnp.float32), 'v_in': jax.random.normal(ks[2], (B, S, D), jnp.float32), 'Wq': jax.random.normal(ks[3], (D, D), jnp.float32) * sc, 'bq': jax.random.normal(ks[4], (D,), jnp.float32) * sc, 'Wk': jax.random.normal(ks[5], (D, D), jnp.float32) * sc, 'bk': jax.random.normal(ks[6], (D,), jnp.float32) * sc, 'Wv': jax.random.normal(ks[7], (D, D), jnp.float32) * sc, 'bv': jax.random.normal(ks[8], (D,), jnp.float32) * sc, 'Wo': jax.random.normal(ks[9], (D, D), jnp.float32) * sc, 'bo': jax.random.normal(ks[10], (D,), jnp.float32) * sc}
    _L0_xattn_all = _L0_xattn_setup()
    _L0_xattn_in = {k: v for k, v in _L0_xattn_all.items() if k in ('Wq', 'bq', 'Wk', 'bk', 'Wv', 'bv', 'Wo', 'bo')}
    del _L0_xattn_all

    def _L0_ffn_setup():
        import jax, jax.numpy as jnp
        import numpy as np
        D_MODEL = 128
        N_EXPERTS = 8
        TOP_K = 2
        key = jax.random.key(seed)
        ks = jax.random.split(key, 8)
        d, e = (D_MODEL, N_EXPERTS)
        s = 1.0 / np.sqrt(d)
        return {'x': jax.random.normal(ks[0], (4, 256, d), dtype=jnp.float32), 'W_gate': jax.random.uniform(ks[1], (d, e), jnp.float32, -s, s), 'b_gate': jax.random.uniform(ks[2], (e,), jnp.float32, -s, s), 'W1': jax.random.uniform(ks[3], (e, d, d), jnp.float32, -s, s), 'b1': jax.random.uniform(ks[4], (e, d), jnp.float32, -s, s), 'W2': jax.random.uniform(ks[5], (e, d, d), jnp.float32, -s, s), 'b2': jax.random.uniform(ks[6], (e, d), jnp.float32, -s, s)}
    _L0_ffn_all = _L0_ffn_setup()
    _L0_ffn_in = {k: v for k, v in _L0_ffn_all.items() if k in ('W_gate', 'b_gate', 'W1', 'b1', 'W2', 'b2')}
    del _L0_ffn_all

    def _L1_xattn_setup():
        import jax, jax.numpy as jnp
        import numpy as np
        D_MODEL = 128
        NUM_HEADS = 16
        HEAD_DIM = D_MODEL // NUM_HEADS
        B, S = (2, 256)

        def _xavier(key, shape, fan_in, fan_out):
            a = jnp.sqrt(6.0 / (fan_in + fan_out)).astype(jnp.float32)
            return jax.random.uniform(key, shape, jnp.float32, -a, a)
        key = jax.random.key(seed)
        ks = jax.random.split(key, 7)
        Q = jax.random.normal(ks[0], (B, S, D_MODEL), jnp.float32)
        K = jax.random.normal(ks[1], (B, S, D_MODEL), jnp.float32)
        V = jax.random.normal(ks[2], (B, S, D_MODEL), jnp.float32)
        Wq = _xavier(ks[3], (NUM_HEADS, D_MODEL, HEAD_DIM), D_MODEL, HEAD_DIM)
        Wk = _xavier(ks[4], (NUM_HEADS, D_MODEL, HEAD_DIM), D_MODEL, HEAD_DIM)
        Wv = _xavier(ks[5], (NUM_HEADS, D_MODEL, HEAD_DIM), D_MODEL, HEAD_DIM)
        Wd = _xavier(ks[6], (D_MODEL, D_MODEL), D_MODEL, D_MODEL)
        return {'Q': Q, 'K': K, 'V': V, 'Wq': Wq, 'Wk': Wk, 'Wv': Wv, 'Wd': Wd}
    _L1_xattn_all = _L1_xattn_setup()
    _L1_xattn_in = {k: v for k, v in _L1_xattn_all.items() if k in ('Wq', 'Wk', 'Wv', 'Wd')}
    del _L1_xattn_all

    def _L1_ffn_setup():
        import jax, jax.numpy as jnp
        import numpy as np
        from jax import lax
        T, B, I, M, O = (32, 64, 128, 128, 128)

        def _xavier(key, shape):
            fan_out, fan_in = shape
            limit = float(np.sqrt(6.0 / (fan_in + fan_out)))
            return jax.random.uniform(key, shape, jnp.float32, -limit, limit)
        key = jax.random.key(seed)
        ks = jax.random.split(key, 9)
        x = jax.random.normal(ks[0], (T, B, I), jnp.float32)
        return {'x': x, 'wf': _xavier(ks[1], (M, I)), 'uf': _xavier(ks[2], (M, M)), 'bf': jnp.zeros((M,), jnp.float32), 'wi': _xavier(ks[3], (M, I)), 'ui': _xavier(ks[4], (M, M)), 'bi': jnp.zeros((M,), jnp.float32), 'wc': _xavier(ks[5], (M, I)), 'uc': _xavier(ks[6], (M, M)), 'bc': jnp.zeros((M,), jnp.float32), 'wo': _xavier(ks[7], (O, I)), 'uo': _xavier(ks[8], (O, M)), 'bo': jnp.zeros((O,), jnp.float32), 'in_c': jnp.zeros((M,), jnp.float32)}
    _L1_ffn_all = _L1_ffn_setup()
    _L1_ffn_in = {k: v for k, v in _L1_ffn_all.items() if k in ('wf', 'uf', 'bf', 'wi', 'ui', 'bi', 'wc', 'uc', 'bc', 'wo', 'uo', 'bo', 'in_c')}
    del _L1_ffn_all
    return {'x': x, 'ctx_1024': ctx_1024, 'L0_xattn_Wq': _L0_xattn_in['Wq'], 'L0_xattn_bq': _L0_xattn_in['bq'], 'L0_xattn_Wk': _L0_xattn_in['Wk'], 'L0_xattn_bk': _L0_xattn_in['bk'], 'L0_xattn_Wv': _L0_xattn_in['Wv'], 'L0_xattn_bv': _L0_xattn_in['bv'], 'L0_xattn_Wo': _L0_xattn_in['Wo'], 'L0_xattn_bo': _L0_xattn_in['bo'], 'L0_ffn_W_gate': _L0_ffn_in['W_gate'], 'L0_ffn_b_gate': _L0_ffn_in['b_gate'], 'L0_ffn_W1': _L0_ffn_in['W1'], 'L0_ffn_b1': _L0_ffn_in['b1'], 'L0_ffn_W2': _L0_ffn_in['W2'], 'L0_ffn_b2': _L0_ffn_in['b2'], 'L1_xattn_Wq': _L1_xattn_in['Wq'], 'L1_xattn_Wk': _L1_xattn_in['Wk'], 'L1_xattn_Wv': _L1_xattn_in['Wv'], 'L1_xattn_Wd': _L1_xattn_in['Wd'], 'L1_ffn_wf': _L1_ffn_in['wf'], 'L1_ffn_uf': _L1_ffn_in['uf'], 'L1_ffn_bf': _L1_ffn_in['bf'], 'L1_ffn_wi': _L1_ffn_in['wi'], 'L1_ffn_ui': _L1_ffn_in['ui'], 'L1_ffn_bi': _L1_ffn_in['bi'], 'L1_ffn_wc': _L1_ffn_in['wc'], 'L1_ffn_uc': _L1_ffn_in['uc'], 'L1_ffn_bc': _L1_ffn_in['bc'], 'L1_ffn_wo': _L1_ffn_in['wo'], 'L1_ffn_uo': _L1_ffn_in['uo'], 'L1_ffn_bo': _L1_ffn_in['bo'], 'L1_ffn_in_c': _L1_ffn_in['in_c']}

def reference(x, ctx_1024, L0_xattn_Wq, L0_xattn_bq, L0_xattn_Wk, L0_xattn_bk, L0_xattn_Wv, L0_xattn_bv, L0_xattn_Wo, L0_xattn_bo, L0_ffn_W_gate, L0_ffn_b_gate, L0_ffn_W1, L0_ffn_b1, L0_ffn_W2, L0_ffn_b2, L1_xattn_Wq, L1_xattn_Wk, L1_xattn_Wv, L1_xattn_Wd, L1_ffn_wf, L1_ffn_uf, L1_ffn_bf, L1_ffn_wi, L1_ffn_ui, L1_ffn_bi, L1_ffn_wc, L1_ffn_uc, L1_ffn_bc, L1_ffn_wo, L1_ffn_uo, L1_ffn_bo, L1_ffn_in_c):
    import jax
    import jax.numpy as jnp

    def _L0_xattn_ref(q_in, k_in, v_in, Wq, bq, Wk, bk, Wv, bv, Wo, bo):
        import jax, jax.numpy as jnp
        import numpy as np
        H = 16
        B, S, D = q_in.shape
        hd = D // H
        q = q_in @ Wq.T + bq
        k = k_in @ Wk.T + bk
        v = v_in @ Wv.T + bv
        q = q.reshape(B, S, H, hd).transpose(0, 2, 1, 3)
        k = k.reshape(B, S, H, hd).transpose(0, 2, 1, 3)
        v = v.reshape(B, S, H, hd).transpose(0, 2, 1, 3)
        scores = jnp.einsum('bhqd,bhkd->bhqk', q, k) / jnp.sqrt(jnp.float32(hd))
        probs = jax.nn.softmax(scores, axis=-1)
        attn = jnp.einsum('bhqk,bhkd->bhqd', probs, v)
        concat = attn.transpose(0, 2, 1, 3).reshape(B, S, D)
        return concat @ Wo.T + bo

    def _L0_ffn_ref(x, W_gate, b_gate, W1, b1, W2, b2):
        import jax, jax.numpy as jnp
        import numpy as np
        D_MODEL = 128
        N_EXPERTS = 8
        TOP_K = 2
        B, T, d = x.shape
        xf = x.reshape(-1, d)
        scores = xf @ W_gate + b_gate
        topk_val, topk_idx = jax.lax.top_k(scores, TOP_K)
        onehot = jax.nn.one_hot(topk_idx, N_EXPERTS, dtype=xf.dtype)
        w = jnp.einsum('nk,nke->ne', topk_val, onehot)
        h = jax.nn.relu(jnp.einsum('nd,edh->neh', xf, W1) + b1)
        y = jnp.einsum('neh,ehd->ned', h, W2) + b2
        out = jnp.einsum('ned,ne->nd', y, w)
        return out.reshape(B, T, d)

    def _L1_xattn_ref(Q, K, V, Wq, Wk, Wv, Wd):
        import jax, jax.numpy as jnp
        import numpy as np
        D_MODEL = 128
        NUM_HEADS = 16
        HEAD_DIM = D_MODEL // NUM_HEADS
        B, S = (2, 256)

        def _xavier(key, shape, fan_in, fan_out):
            a = jnp.sqrt(6.0 / (fan_in + fan_out)).astype(jnp.float32)
            return jax.random.uniform(key, shape, jnp.float32, -a, a)
        q = jnp.einsum('bsd,hdk->bhsk', Q, Wq)
        k = jnp.einsum('btd,hdk->bhtk', K, Wk)
        v = jnp.einsum('btd,hdk->bhtk', V, Wv)
        scale = 1.0 / jnp.sqrt(jnp.asarray(HEAD_DIM, q.dtype))
        scores = jnp.einsum('bhsk,bhtk->bhst', q, k) * scale
        attn = jax.nn.softmax(scores, axis=-1)
        ctx = jnp.einsum('bhst,bhtk->bhsk', attn, v)
        concat = jnp.transpose(ctx, (0, 2, 1, 3)).reshape(ctx.shape[0], ctx.shape[2], -1)
        out = jnp.einsum('bsd,ed->bse', concat, Wd)
        return out

    def _L1_ffn_ref(x, wf, uf, bf, wi, ui, bi, wc, uc, bc, wo, uo, bo, in_c):
        import jax, jax.numpy as jnp
        import numpy as np
        from jax import lax
        T, B, I, M, O = (32, 64, 128, 128, 128)

        def _xavier(key, shape):
            fan_out, fan_in = shape
            limit = float(np.sqrt(6.0 / (fan_in + fan_out)))
            return jax.random.uniform(key, shape, jnp.float32, -limit, limit)
        batch = x.shape[1]
        c0 = jnp.broadcast_to(in_c, (batch, in_c.shape[0]))

        def step(c, xt):
            ft = jax.nn.sigmoid(xt @ wf.T + c @ uf.T + bf)
            it = jax.nn.sigmoid(xt @ wi.T + c @ ui.T + bi)
            gt = jnp.tanh(xt @ wc.T + c @ uc.T + bc)
            c = ft * c + it * gt
            return (c, None)
        c_final, _ = lax.scan(step, c0, x)
        h = jnp.tanh(jnp.einsum('tbi,oi->tbo', x, wo) + c_final @ uo.T + bo)
        return h
    x = x + _L0_xattn_ref(_layernorm(x, axis=-1), ctx_1024, ctx_1024, L0_xattn_Wq, L0_xattn_bq, L0_xattn_Wk, L0_xattn_bk, L0_xattn_Wv, L0_xattn_bv, L0_xattn_Wo, L0_xattn_bo)
    x = x + _L0_ffn_ref(_layernorm(x, axis=-1), L0_ffn_W_gate, L0_ffn_b_gate, L0_ffn_W1, L0_ffn_b1, L0_ffn_W2, L0_ffn_b2)
    x = x + _L1_xattn_ref(_layernorm(x, axis=-1), ctx_1024, ctx_1024, L1_xattn_Wq, L1_xattn_Wk, L1_xattn_Wv, L1_xattn_Wd)
    x = x + _L1_ffn_ref(_layernorm(x, axis=-1), L1_ffn_wf, L1_ffn_uf, L1_ffn_bf, L1_ffn_wi, L1_ffn_ui, L1_ffn_bi, L1_ffn_wc, L1_ffn_uc, L1_ffn_bc, L1_ffn_wo, L1_ffn_uo, L1_ffn_bo, L1_ffn_in_c)
    return x

_drawn_inputs = setup_inputs


def setup_inputs(seed=0):
    import zlib

    import numpy as np

    out = dict(_drawn_inputs(seed))
    spreads = {'L1_ffn_bf': (0.0, 0.8),
     'L1_ffn_bi': (0.0, 0.8),
     'L1_ffn_bc': (0.0, 0.1),
     'L1_ffn_bo': (0.0, 0.1),
     'L1_ffn_in_c': (0.0, 0.8)}
    factors = {'L0_xattn_Wq': 8.0,
     'L0_xattn_bq': 25.209,
     'L0_xattn_Wk': 8.0,
     'L0_xattn_bk': 64.0,
     'L0_xattn_bv': 4.286}
    for name, (base, spread) in spreads.items():
        noise = np.random.default_rng([zlib.crc32(name.encode()), seed]).standard_normal(out[name].shape)
        drawn = base * np.exp(spread * noise) if base else spread * noise
        out[name] = jnp.asarray(drawn.astype(out[name].dtype))
    for name, factor in factors.items():
        out[name] = (out[name] * factor).astype(out[name].dtype)
    return out
```

```python
from contextlib import ExitStack

import numpy as np

import concourse.bass as bass
from concourse import mybir

P = 128
NT = 64
H = 16
E = 8
EPS = 1e-5
SCALE = 1.0 / float(np.sqrt(8.0))
F32 = mybir.dt.float32
U32 = mybir.dt.uint32
ALU = mybir.AluOpType
ACT = mybir.ActivationFunctionType
AX = mybir.AxisListType

LOADS = [1, 1, 2, 4, 8, 8, 8, 8, 8, 8, 8]
TAIL = 8


class Queue:

    def __init__(self, sem):
        self.sem = sem
        self.count = 0
        self.seen = {}
        self.ops = []

    def op(self, fn):
        self.ops.append(fn)

    def done(self, fn):
        sem = self.sem
        self.count += 1
        self.ops.append(lambda e: fn(e).then_inc(sem, 1))
        return (sem, self.count)

    def dma(self, fn, sem):
        self.ops.append(lambda e: fn(e).then_inc(sem, 16))

    def need(self, *marks):
        for sem, value in marks:
            key = sem.name
            if self.seen.get(key, 0) < value:
                self.seen[key] = value
                self.ops.append(lambda e, s=sem, v=value: e.wait_ge(s, v))

    def run(self, e):
        for fn in self.ops:
            fn(e)


def build(nc, a, const, out):
    ctx = ExitStack()
    with ctx:
        def sb(name, shape, dt=F32):
            return ctx.enter_context(nc.sbuf_tensor(name, shape, dt))

        def sem(name):
            return ctx.enter_context(nc.semaphore(name))

        pe, dve, act, pool, sp = (Queue(sem(n)) for n in ("s_pe", "s_dve", "s_act", "s_pool", "s_sp"))

        x = sb("x", [P, NT, 128])
        cx = sb("cx", [P, NT, 128])
        cst = sb("cst", [P, 128 + 8 + 8 + 16])
        ident = cst[:, 0:128]
        hmask = cst[:, 128:136]
        iota = cst[:, 136:144]
        wst = sb("wst", [P, 13, 128])
        wT = sb("wT", [P, 13, 128])
        wq1 = sb("wq1", [P, 128])
        wk1 = sb("wk1", [P, 128])
        wv1 = sb("wv1", [P, 128])
        wg = sb("wg", [P, 8])
        w1 = sb("w1", [P, E, 128])
        w2 = sb("w2", [P, E, 128])
        b2 = sb("b2", [E, 128])
        col = sb("col", [P, 24])
        bo0 = sb("bo0", [P, 128])
        bo1 = sb("bo1", [P, 128])
        bg = sb("bg", [P, 8])
        xn = sb("xn", [P, 8, 128])
        st = sb("st", [P, 8, 6])
        mv = sb("mv", [P, 8, 2])
        ve = sb("ve", [P, 8, 1])
        rs = sb("rs", [P, 8, 1])
        xT = sb("xT", [P, 8, 128])
        qT = sb("qT", [P, 4, 128])
        kT = sb("kT", [P, 2, 128])
        Km = sb("Km", [P, 4, 8, 128])
        Vb = sb("Vb", [P, 8, 2, 8, 32])
        mx = sb("mx", [P, 4, 16])
        Ex = sb("Ex", [P, 4, 1024])
        ET = sb("ET", [P, 4, 8, 128])
        raw = sb("raw", [P, 4, 256])
        rd = sb("rd", [P, 4, 16])
        att = sb("att", [P, 4, 128])
        aT = sb("aT", [P, 4, 128])
        hT = sb("hT", [P, 2, E, 128])
        sc = sb("sc", [P, 2, 8])
        top = sb("top", [P, 2, 8])
        tix = sb("tix", [P, 2, 8], U32)
        tif = sb("tif", [P, 2, 2])
        wa = sb("wa", [P, 2, 8])
        wb = sb("wb", [P, 2, 8])
        we = sb("we", [P, 2, 8])
        weT = sb("weT", [E, 2, 128])
        acc = sb("acc", [P, 2, 2, 128])
        TG = sb("TG", [P, 2, 128])
        CG = sb("CG", [P, 3, 128])
        AB = sb("AB", [P, 2, 128])
        cU = sb("cU", [P, 128])

        banks = [ctx.enter_context(nc.psum_tensor(f"ps{i}", [P, 512], F32)) for i in range(8)]
        lstm = banks[7]
        ring = [[] for _ in range(7)]
        turn = [0]

        def bank():
            i = turn[0] % 7
            turn[0] += 1
            pe.need(*ring[i])
            ring[i] = []
            return i, banks[i]

        def free(i, mark):
            ring[i].append(mark)

        x_v = a["x"].rearrange("a b d -> (a b) d").rearrange("(t p) d -> p t d", p=P)
        c_v = a["ctx_1024"].rearrange("a b d -> (a b) d").rearrange("(t p) d -> p t d", p=P)
        o_v = out.rearrange("a b d -> (a b) d").rearrange("(t p) d -> p t d", p=P)
        x_in, c_in = {}, {}
        starts = np.cumsum([0] + LOADS)

        def load(q, name, fn):
            s = sem("l_" + name)
            q.dma(fn, s)
            return (s, 16)

        def load_x(c):
            t0, t1 = int(starts[c]), int(starts[c + 1])
            m = load(sp, f"x{c}", lambda e: e.dma_start(x[:, t0:t1, :], x_v[:, t0:t1, :]))
            for t in range(t0, t1):
                x_in[t] = m

        def load_c(c):
            t0, t1 = int(starts[c]), int(starts[c + 1])
            m = load(sp, f"c{c}", lambda e: e.dma_start(cx[:, t0:t1, :], c_v[:, t0:t1, :]))
            for t in range(t0, t1):
                c_in[t] = m

        def column(ap):
            return ap.rearrange("(n a) -> n a", a=1)

        def row(ap):
            return ap.rearrange("(a n) -> a n", a=1)

        W = {}
        in_const = load(act, "const", lambda e: e.dma_start(cst[:, :], const))
        load_x(0)
        load_c(0)
        squares = ["L0_xattn_Wq", "L0_xattn_Wk", "L0_xattn_Wv", "L0_xattn_Wo", "L1_xattn_Wd",
                   "L1_ffn_wf", "L1_ffn_wi", "L1_ffn_wc", "L1_ffn_uf", "L1_ffn_ui", "L1_ffn_uc",
                   "L1_ffn_wo", "L1_ffn_uo"]
        factor = {"L1_ffn_wf": 0.5, "L1_ffn_wi": 0.5, "L1_ffn_uf": 0.25, "L1_ffn_ui": 0.25,
                  "L1_ffn_uc": 0.5, "L1_ffn_uo": 0.5}

        def square(n):
            return load(act if n < 2 else sp, f"sq{n}", lambda e: e.dma_start(wst[:, n, :], a[squares[n]]))

        in_sq = [square(n) for n in range(4)]
        BQ, BK, BV, B1, BF, BI, BC, CI = 0, 1, 2, 3, 11, 12, 13, 14
        cols = {"L0_xattn_bq": BQ, "L0_xattn_bk": BK, "L0_xattn_bv": BV, "L1_ffn_bf": BF,
                "L1_ffn_bi": BI, "L1_ffn_bc": BC, "L1_ffn_in_c": CI}

        def load_col(name):
            c = cols[name]
            return load(pool, name, lambda e: e.dma_start(col[:, c:c + 1], column(a[name])))

        in_col = {n: load_col(n) for n in ("L0_xattn_bq", "L0_xattn_bk", "L0_xattn_bv")}
        in_bo0 = load(pool, "bo0", lambda e: e.dma_start(bo0[:, :], row(a["L0_xattn_bo"]).to_broadcast([P, 128])))
        load_x(1)
        load_c(1)
        load_x(2)
        load_c(2)
        for c in range(3, 5):
            load_x(c)
            load_c(c)

        def heads(name, tile):
            return load(sp, name, lambda e: e.dma_start(tile[:, :].rearrange("d (h k) -> d h k", h=H),
                                                        a[name].rearrange("h d k -> d h k")))

        in_k1 = heads("L1_xattn_Wk", wk1)
        in_v1 = heads("L1_xattn_Wv", wv1)
        in_wg = load(pool, "wg", lambda e: e.dma_start(wg[:, :], a["L0_ffn_W_gate"]))
        in_bg = load(pool, "bg", lambda e: e.dma_start(bg[:, :], row(a["L0_ffn_b_gate"]).to_broadcast([P, 8])))
        in_w1 = load(sp, "w1", lambda e: e.dma_start(w1[:, :, :], a["L0_ffn_W1"].rearrange("e d h -> d e h")))
        in_b1 = load(pool, "b1", lambda e: e.dma_start(col[:, B1:B1 + E], a["L0_ffn_b1"].rearrange("e h -> h e"),
                                                                 allow_slow_non_contiguous=True))
        in_w2 = load(sp, "w2", lambda e: e.dma_start(w2[:, :, :], a["L0_ffn_W2"].rearrange("e d h -> d e h")))
        in_b2 = load(pool, "b2", lambda e: e.dma_start(b2[:, :], a["L0_ffn_b2"]))
        in_q1 = heads("L1_xattn_Wq", wq1)
        in_sq += [square(n) for n in range(4, 13)]
        for n in ("L1_ffn_bf", "L1_ffn_bi", "L1_ffn_bc", "L1_ffn_in_c"):
            in_col[n] = load_col(n)
        in_bo1 = load(pool, "bo1", lambda e: e.dma_start(bo1[:, :], row(a["L1_ffn_bo"]).to_broadcast([P, 128])))
        for c in range(5, len(LOADS)):
            load_x(c)
            load_c(c)

        z = pool.done(lambda e: e.memset(Vb[:, :, :, :, :], 0.0))
        pool.need(z)
        z = pool.done(lambda e: e.memset(Vb[0:64, :, :, :, 16:17], 1.0))
        pool.need(z)
        vb_set = pool.done(lambda e: e.memset(Vb[64:128, :, :, :, 17:18], 1.0))
        half = sb("half", [P, 1])
        pool.need(vb_set)
        half_set = pool.done(lambda e: e.memset(half[:, :], -0.5))

        w_ready = {}

        def turn_weight(n):
            i, b = bank()
            pe.need(in_const, in_sq[n])
            m = pe.done(lambda e: e.transpose(b[:, 0:128], wst[:, n, :], ident))
            act.need(m)
            f = factor.get(squares[n], 1.0)
            m = act.done(lambda e: e.activation(wT[:, n, :], b[:, 0:128], ACT.Copy, scale=f))
            free(i, m)
            w_ready[n] = m

        WQ, WK, WV, WO, WD, WF, WI, WC, UF, UI, UC, WX, UO = range(13)

        M = {}

        def ctx_turn(t):
            i, b = bank()
            pe.need(in_const, c_in[t])
            m = pe.done(lambda e: e.transpose(b[:, 0:128], cx[:, t, :], ident))
            act.need(m)
            M["cT", t] = act.done(lambda e: e.activation(cx[:, t, :], b[:, 0:128], ACT.Copy))
            free(i, M["cT", t])

        def keys_values(L, t):
            i, b = bank()
            wk, wv = (wT[:, WK, :], wT[:, WV, :]) if L == 0 else (wk1[:, :], wv1[:, :])
            pe.need(M["cT", t])
            pe.need(*((w_ready[WK], w_ready[WV]) if L == 0 else (in_k1, in_v1)))
            k = pe.done(lambda e: e.matmul(b[:, 0:128], wk, cx[:, t, :], start=True, stop=True))
            wv2 = wv.rearrange("p (n two d) -> p two n d", two=2, d=8)
            for s in range(2):
                for h in range(2):
                    fn = (lambda e, s=s, h=h: e.matmul(b[64 * h:64 * h + 64, 128 + 64 * s:192 + 64 * s],
                                                       cx[:, t, 64 * s:64 * s + 64], wv2[:, h, :, :],
                                                       start=True, stop=True, skip_group_check=True))
                    if (s, h) == (1, 1):
                        v = pe.done(fn)
                    else:
                        pe.op(fn)
            vs = 4 * L + t % 4
            act.need(v)
            act.need(vb_set)
            if t >= 4:
                act.need(M["pv", L, t - 4])
            for h in range(2):
                src = b[64 * h:64 * h + 64, 128:256].rearrange("p (s n d) -> p s n d", s=2, d=8)
                dst = Vb[64 * h:64 * h + 64, vs, :, :, 8 * h:8 * h + 8]
                m = act.done(lambda e, src=src, dst=dst: e.activation(dst, src, ACT.Copy))
            M["V", L, t] = m
            if t >= 1:
                act.need(M["K", L, t - 1])
            if L == 0:
                act.need(in_col["L0_xattn_bk"])
                m = act.done(lambda e: e.activation(kT[:, L, :], b[:, 0:128], ACT.Identity,
                                                    bias=col[:, BK:BK + 1]))
            else:
                m = act.done(lambda e: e.activation(kT[:, L, :], b[:, 0:128], ACT.Copy))
            free(i, m)
            pool.need(in_const, m)
            if t >= 2:
                pool.need(M["S", L, t - 2])
            M["K", L, t] = pool.done(lambda e: e.tensor_tensor(
                Km[:, 2 * L + t % 2, :, :], kT[:, L, :].unsqueeze(1).to_broadcast([P, 8, 128]),
                hmask.unsqueeze(2).to_broadcast([P, 8, 128]), ALU.mult))

        def norm(k, t, src):
            s = 2 * k + t % 2
            dve.need(*src)
            m = dve.done(lambda e: e.bn_stats(st[:, s, :], x[:, t, :]))
            dve.need(m)
            if t >= 2:
                dve.need(M["n", k, t - 2])
            m = dve.done(lambda e: e.bn_aggr(mv[:, s, :], st[:, s, :]))
            pool.need(m, half_set)
            m = pool.done(lambda e: e.tensor_scalar(ve[:, s, :], mv[:, s, 1:2], EPS, None, ALU.add))
            pool.need(m)
            m = pool.done(lambda e: e.tensor_tensor(rs[:, s, :], ve[:, s, :], half[:, :], ALU.pow))
            pool.need(m)
            if t >= 2:
                pool.need(M["xn_read", k, t - 2])
            return pool.done(lambda e: e.tensor_scalar(xn[:, s, :], x[:, t, :], mv[:, s, 0:1], rs[:, s, :],
                                                    ALU.subtract, ALU.mult))

        def turn_x(t, k):
            s = 2 * k + t % 2
            i, b = bank()
            pe.need(M["n", k, t])
            m = pe.done(lambda e: e.transpose(b[:, 0:128], xn[:, s, :], ident))
            M["xn_read", k, t] = m
            act.need(m)
            if t >= 2:
                act.need(M["xT_read", k, t - 2])
            m = act.done(lambda e: e.activation(xT[:, s, :], b[:, 0:128], ACT.Copy))
            free(i, m)
            M["xT", k, t] = m

        def query(L, t):
            s = t % 2
            i, b = bank()
            pe.need(M["xT", 2 * L, t])
            pe.need(w_ready[WQ] if L == 0 else in_q1)
            w = wT[:, WQ, :] if L == 0 else wq1[:, :]
            m = pe.done(lambda e: e.matmul(b[:, 0:128], w, xT[:, 4 * L + s, :], start=True, stop=True))
            M["xT_read", 2 * L, t] = m
            act.need(m)
            if t >= 2:
                act.need(M["S", L, t - 2])
            if L == 0:
                act.need(in_col["L0_xattn_bq"])
                m = act.done(lambda e: e.activation(qT[:, s, :], b[:, 0:128], ACT.Identity,
                                                    bias=col[:, BQ:BQ + 1]))
            else:
                m = act.done(lambda e: e.activation(qT[:, 2 + s, :], b[:, 0:128], ACT.Copy))
            free(i, m)
            M["q", L, t] = m

        def scores(L, t):
            s = 2 * L + t % 2
            pe.need(M["q", L, t], M["K", L, t])
            (i0, b0), (i1, b1) = bank(), bank()
            marks = []
            for r, b in ((0, b0), (1, b1)):
                for n in range(2):
                    fn = (lambda e, r=r, b=b, n=n: e.matmul(
                        b[64 * n:64 * n + 64, :].rearrange("p (j k) -> p j k", j=8),
                        qT[64 * r:64 * r + 64, s, 64 * n:64 * n + 64],
                        Km[64 * r:64 * r + 64, s, :, 64 * n:64 * n + 64],
                        start=True, stop=True, skip_group_check=True))
                    if n:
                        marks.append(pe.done(fn))
                    else:
                        pe.op(fn)
            M["S", L, t] = marks[1]
            if t >= 2:
                dve.need(M["ET_mm", L, t - 2])
            for r, (i, b) in enumerate(((i0, b0), (i1, b1))):
                S = b[:, :].rearrange("p (j k) -> p j k", j=8)
                mr = mx[:, s, 8 * r:8 * r + 8]
                Er = Ex[:, s, 512 * r:512 * r + 512]
                dve.need(marks[r])
                m = dve.done(lambda e, S=S, mr=mr: e.tensor_reduce(mr, S, AX.X, ALU.max))
                dve.need(m)
                m = dve.done(lambda e, S=S, mr=mr, Er=Er: e.tensor_tensor(
                    Er.rearrange("p (j k) -> p j k", j=8), S,
                    mr.unsqueeze(2).to_broadcast([P, 8, 64]), ALU.subtract))
                free(i, m)
                act.need(m)
                M["E%d" % r, L, t] = act.done(lambda e, Er=Er: e.activation(Er, Er, ACT.Exp, scale=SCALE))

        def turn_e(L, t):
            s = 2 * L + t % 2
            for r in range(2):
                i, b = bank()
                pe.need(M["E%d" % r, L, t])
                for n in range(4):
                    g = 4 * r + n
                    fn = (lambda e, n=n, g=g, b=b: e.transpose(b[:, 128 * n:128 * n + 128],
                                                               Ex[:, s, 128 * g:128 * g + 128], ident))
                    if n == 3:
                        m = pe.done(fn)
                    else:
                        pe.op(fn)
                act.need(m)
                if t >= 2:
                    act.need(M["pv", L, t - 2])
                M["ET%d" % r, L, t] = act.done(lambda e, b=b, r=r: e.activation(
                    ET[:, s, 4 * r:4 * r + 4, :], b[:, :].rearrange("p (n q) -> p n q", n=4), ACT.Copy))
                free(i, M["ET%d" % r, L, t])
            M["ET_mm", L, t] = m

        def values(L, t):
            s = 2 * L + t % 2
            vs = 4 * L + t % 4
            i, b = bank()
            pe.need(M["ET0", L, t], M["ET1", L, t], M["V", L, t])
            for n in range(2):
                for g in range(8):
                    j, c = g % 4, g // 4
                    fn = (lambda e, n=n, g=g, j=j, c=c: e.matmul(
                        b[32 * j:32 * j + 32, 128 * c + 64 * n:128 * c + 64 * n + 64],
                        Vb[:, vs, n, g, :], ET[:, s, g, 64 * n:64 * n + 64],
                        start=True, stop=True, skip_group_check=True))
                    if (n, g) == (1, 7):
                        m = pe.done(fn)
                    else:
                        pe.op(fn)
            M["pv", L, t] = m
            act.need(m)
            if t >= 2:
                act.need(M["raw_mm", L, t - 2])
            M["raw", L, t] = act.done(lambda e: e.activation(raw[:, s, :], b[:, 0:256], ACT.Copy))
            free(i, M["raw", L, t])

        def turn_o(L, t):
            s = 2 * L + t % 2
            i, b = bank()
            pe.need(M["raw", L, t])
            pe.op(lambda e: e.transpose(b[:, 0:128], raw[:, s, 0:128], ident))
            m = pe.done(lambda e: e.transpose(b[:, 128:256], raw[:, s, 128:256], ident))
            M["raw_mm", L, t] = m
            o = b[:, 0:256].rearrange("p (g r) -> p g r", r=32)
            dve.need(m)
            m = dve.done(lambda e: e.reciprocal(rd[:, s, :].rearrange("p (g two) -> p g two", two=2),
                                                o[:, :, 16:18]))
            dve.need(m)
            if t >= 2:
                dve.need(M["att_mm", L, t - 2])
            M["att", L, t] = dve.done(lambda e: e.tensor_tensor(
                att[:, s, :].rearrange("p (g two d) -> p g two d", two=2, d=8),
                o[:, :, 0:16].rearrange("p g (two d) -> p g two d", two=2),
                rd[:, s, :].rearrange("p (g two) -> p g two", two=2).unsqueeze(3).to_broadcast([P, 8, 2, 8]),
                ALU.mult))
            free(i, M["att", L, t])

        def turn_a(L, t):
            s = 2 * L + t % 2
            i, b = bank()
            pe.need(M["att", L, t])
            m = pe.done(lambda e: e.transpose(b[:, 0:128], att[:, s, :], ident))
            M["att_mm", L, t] = m
            act.need(m)
            if t >= 2:
                act.need(M["o_mm", L, t - 2])
            if L == 0:
                act.need(in_col["L0_xattn_bv"])
                m = act.done(lambda e: e.activation(aT[:, s, :], b[:, 0:128], ACT.Identity,
                                                    bias=col[:, BV:BV + 1]))
            else:
                m = act.done(lambda e: e.activation(aT[:, s, :], b[:, 0:128], ACT.Copy))
            free(i, m)
            M["aT", L, t] = m

        def project(L, t):
            s = 2 * L + t % 2
            n = WO if L == 0 else WD
            i, b = bank()
            pe.need(M["aT", L, t], w_ready[n])
            m = pe.done(lambda e: e.matmul(b[:, 0:128], aT[:, s, :], wT[:, n, :], start=True, stop=True))
            M["o_mm", L, t] = m
            dve.need(m)
            if L == 0:
                dve.need(M["xb", t])
            m = dve.done(lambda e: e.tensor_tensor(x[:, t, :], b[:, 0:128], x[:, t, :], ALU.add))
            free(i, m)
            M["x_attn", L, t] = m
            M["n", 1 + 2 * L, t] = norm(1 + 2 * L, t, [m])

        def start_x(t):
            M["n", 0, t] = norm(0, t, [x_in[t]])
            pool.need(in_bo0)
            pool.need(M["n", 0, t])
            M["xb", t] = pool.done(lambda e: e.tensor_tensor(x[:, t, :], x[:, t, :], bo0[:, :], ALU.add))

        def gate(t):
            s = t % 2
            i, b = bank()
            pe.need(M["xT", 1, t], in_wg)
            m = pe.done(lambda e: e.matmul(b[:, 0:8], xT[:, 2 + s, :], wg[:, :], start=True, stop=True))
            dve.need(m, in_bg)
            m = dve.done(lambda e: e.tensor_tensor(sc[:, s, :], b[:, 0:8], bg[:, :], ALU.add))
            free(i, m)
            dve.need(m)
            m = dve.done(lambda e: e.max(top[:, s, :], sc[:, s, :]))
            dve.need(m)
            m = dve.done(lambda e: e.max_index(tix[:, s, :], top[:, s, :], sc[:, s, :]))
            dve.need(m)
            m = dve.done(lambda e: e.tensor_copy(tif[:, s, :], tix[:, s, 0:2]))
            dve.need(m, in_const)
            m = dve.done(lambda e: e.tensor_scalar(wa[:, s, :], iota, tif[:, s, 0:1], top[:, s, 0:1],
                                                   ALU.is_equal, ALU.mult))
            m = dve.done(lambda e: e.tensor_scalar(wb[:, s, :], iota, tif[:, s, 1:2], top[:, s, 1:2],
                                                   ALU.is_equal, ALU.mult))
            dve.need(m)
            if t >= 2:
                dve.need(M["we_mm", t - 2])
            M["we", t] = dve.done(lambda e: e.tensor_tensor(we[:, s, :], wa[:, s, :], wb[:, s, :], ALU.add))

        def hidden(t):
            s = t % 2
            pe.need(M["xT", 1, t], in_w1)
            act.need(in_b1)
            for c in range(2):
                i, b = bank()
                for n in range(4):
                    fn = (lambda e, b=b, c=c, n=n: e.matmul(b[:, 128 * n:128 * n + 128], w1[:, 4 * c + n, :],
                                                            xT[:, 2 + s, :], start=True, stop=True,
                                                            skip_group_check=True))
                    if n == 3:
                        m = pe.done(fn)
                    else:
                        pe.op(fn)
                act.need(m)
                if t >= 2:
                    act.need(M["y_mm%d" % c, t - 2])
                for n in range(4):
                    k = 4 * c + n
                    fn = (lambda e, b=b, n=n, k=k: e.activation(hT[:, s, k, :], b[:, 128 * n:128 * n + 128],
                                                                ACT.Relu, bias=col[:, B1 + k:B1 + k + 1]))
                    if n == 3:
                        M["h%d" % c, t] = act.done(fn)
                    else:
                        act.op(fn)
                free(i, M["h%d" % c, t])
            M["xT_read", 1, t] = m

        def turn_w(t):
            s = t % 2
            i, b = bank()
            pe.need(M["we", t])
            m = pe.done(lambda e: e.transpose(b[0:8, 0:128], we[:, s, :], ident))
            M["we_mm", t] = m
            act.need(m)
            if t >= 2:
                act.need(M["b2_mm", t - 2])
            M["weT", t] = act.done(lambda e: e.activation(weT[:, s, :], b[0:8, 0:128], ACT.Copy))
            free(i, M["weT", t])

        def experts(t):
            s = t % 2
            held = []
            for c in range(2):
                i, b = bank()
                pe.need(M["h%d" % c, t], in_w2)
                for n in range(4):
                    k = 4 * c + n
                    fn = (lambda e, b=b, k=k, n=n: e.matmul(b[:, 128 * n:128 * n + 128], hT[:, s, k, :],
                                                            w2[:, k, :], start=True, stop=True,
                                                            skip_group_check=True))
                    if n == 3:
                        m = pe.done(fn)
                    else:
                        pe.op(fn)
                M["y_mm%d" % c, t] = m
                held.append((i, b, m))
            i2, bb = bank()
            pe.need(M["weT", t], in_b2)
            mb = pe.done(lambda e: e.matmul(bb[:, 0:128], weT[:, s, :], b2[:, :], start=True, stop=True))
            M["b2_mm", t] = mb
            last = [None, None]
            for n in range(4):
                for c in range(2):
                    i, b, m = held[c]
                    dve.need(m)
                    k = 4 * c + n
                    y = b[:, 128 * n:128 * n + 128]
                    w = we[:, s, k:k + 1]
                    d = acc[:, s, c, :]
                    if n == 0 and c == 1:
                        last[1] = dve.done(lambda e, y=y, w=w, d=d: e.tensor_scalar(d, y, w, None, ALU.mult))
                        continue
                    src = x[:, t, :] if n == 0 else d
                    if n:
                        dve.need(last[c])
                    last[c] = dve.done(lambda e, y=y, w=w, d=d, src=src: e.scalar_tensor_tensor(
                        d, y, w, src, ALU.mult, ALU.add))
            for c in range(2):
                free(held[c][0], last[c])
            dve.need(mb, last[1])
            m = dve.done(lambda e: e.tensor_tensor(acc[:, s, 1, :], bb[:, 0:128], acc[:, s, 1, :], ALU.add))
            free(i2, m)
            dve.need(m)
            m = dve.done(lambda e: e.tensor_tensor(x[:, t, :], acc[:, s, 0, :], acc[:, s, 1, :], ALU.add))
            M["x_moe", t] = m
            M["n", 2, t] = norm(2, t, [m])

        def inputs(t):
            s = t % 2
            i, b = bank()
            pe.need(M["xT", 3, t], w_ready[WX], w_ready[WF], w_ready[WI], w_ready[WC])
            m = pe.done(lambda e: e.matmul(b[:, 0:128], xT[:, 6 + s, :], wT[:, WX, :], start=True, stop=True))
            act.need(m)
            act.need(M["V", 1, t])
            M["xo", t] = act.done(lambda e: e.activation(cx[:, t, :], b[:, 0:128], ACT.Copy))
            free(i, M["xo", t])
            if t:
                pe.need(M["gates", 2 * t - 1])
            for n, w in enumerate((WF, WI, WC)):
                fn = (lambda e, n=n, w=w: e.matmul(lstm[:, 128 * n:128 * n + 128], wT[:, w, :], xT[:, 6 + s, :],
                                                   start=(n == 0), stop=False, skip_group_check=True))
                if n == 2:
                    M["xT_read", 3, t] = pe.done(fn)
                else:
                    pe.op(fn)

        def step(k):
            t, o = k // 2, 64 * (k % 2)
            pe.need(M["C", k - 1], w_ready[UF], w_ready[UI], w_ready[UC])
            c_in_now = CG[:, k % 3, 0:64]
            for n, w in enumerate((UF, UI, UC)):
                fn = (lambda e, n=n, w=w: e.matmul(lstm[:, 128 * n + o:128 * n + o + 64], wT[:, w, :], c_in_now,
                                                   start=False, stop=True, skip_group_check=True))
                if n == 2:
                    m = pe.done(fn)
                else:
                    pe.op(fn)
            act.need(m)
            if k >= 2:
                act.need(M["AB", k - 2])
            act.need(cols_half, in_col["L1_ffn_bc"])
            if k >= 3:
                act.need(M["AB", k - 3])
            act.op(lambda e: e.activation(TG[:, k % 2, 0:64], lstm[:, o:o + 64], ACT.Tanh, bias=col[:, BF + 4:BF + 5]))
            act.op(lambda e: e.activation(TG[:, k % 2, 64:128], lstm[:, 128 + o:192 + o], ACT.Tanh,
                                          bias=col[:, BF + 5:BF + 6]))
            M["gates", k] = act.done(lambda e: e.activation(CG[:, k % 3, 64:128], lstm[:, 256 + o:320 + o],
                                                            ACT.Tanh, bias=col[:, BC:BC + 1]))
            dve.need(M["gates", k], M["C", k - 1])
            M["AB", k] = dve.done(lambda e: e.scalar_tensor_tensor(AB[:, k % 2, :], TG[:, k % 2, :], 1.0,
                                                                   CG[:, k % 3, :], ALU.add, ALU.mult))
            dve.need(M["AB", k])
            M["C", k] = dve.done(lambda e: e.scalar_tensor_tensor(CG[:, (k + 1) % 3, 0:64], AB[:, k % 2, 0:64], 0.5,
                                                                  AB[:, k % 2, 64:128], ALU.mult, ALU.add))

        for n in (WQ, WK, WV, WO):
            turn_weight(n)
        late = {3: list(range(4, 13))}

        stages = [
            (lambda t: step(2 * t), 22),
            (lambda t: ctx_turn(t), 0),
            (lambda t: start_x(t), 0),
            (lambda t: keys_values(0, t), 2),
            (lambda t: turn_x(t, 0), 1),
            (lambda t: query(0, t), 2),
            (lambda t: scores(0, t), 3),
            (lambda t: turn_e(0, t), 4),
            (lambda t: values(0, t), 5),
            (lambda t: turn_o(0, t), 6),
            (lambda t: turn_a(0, t), 7),
            (lambda t: project(0, t), 8),
            (lambda t: turn_x(t, 1), 9),
            (lambda t: gate(t), 10),
            (lambda t: hidden(t), 10),
            (lambda t: step(2 * t + 1), 22),
            (lambda t: turn_w(t), 11),
            (lambda t: keys_values(1, t), 13),
            (lambda t: experts(t), 11),
            (lambda t: turn_x(t, 2), 12),
            (lambda t: query(1, t), 13),
            (lambda t: scores(1, t), 14),
            (lambda t: turn_e(1, t), 15),
            (lambda t: values(1, t), 16),
            (lambda t: turn_o(1, t), 17),
            (lambda t: turn_a(1, t), 18),
            (lambda t: project(1, t), 19),
            (lambda t: turn_x(t, 3), 20),
            (lambda t: inputs(t), 21),
        ]

        cols_half = None

        def recurrent_setup():
            act.need(in_col["L1_ffn_bf"], in_col["L1_ffn_bi"], in_col["L1_ffn_in_c"])
            m = act.done(lambda e: e.activation(col[:, BF + 4:BF + 6], col[:, BF:BF + 2], ACT.Copy, scale=0.5))
            M["C", -1] = act.done(lambda e: e.activation(CG[:, 0, 0:64], col[:, CI:CI + 1].to_broadcast([P, 64]),
                                                         ACT.Copy, scale=2.0))
            return m

        total = NT + 23
        for it in range(total):
            if it in late:
                for n in late[it]:
                    turn_weight(n)
                cols_half = recurrent_setup()
            for fn, lag in stages:
                t = it - lag
                if 0 <= t < NT:
                    fn(t)

        i, b = bank()
        K = 2 * NT - 1
        pe.need(M["C", K], w_ready[UO])
        pe.op(lambda e: e.matmul(b[0:64, 0:128], CG[:, (K + 1) % 3, 0:64], wT[:, UO, :], start=True, stop=True))
        m = pe.done(lambda e: e.matmul(b[64:128, 0:128], CG[:, (K + 1) % 3, 0:64], wT[:, UO, :],
                                       start=True, stop=True, skip_group_check=True))
        dve.need(m, in_bo1)
        cu = dve.done(lambda e: e.tensor_tensor(cU[:, :], b[:, 0:128], bo1[:, :], ALU.add))
        s_out = sem("s_out")
        n_out = 0
        for c in range(NT // TAIL):
            ts = slice(TAIL * c, TAIL * c + TAIL)
            adder = pool if c % 4 == 3 else dve
            adder.need(cu, M["xo", NT - 1])
            m = adder.done(lambda e, ts=ts: e.tensor_tensor(
                cx[:, ts, :], cx[:, ts, :], cU[:, :].unsqueeze(1).to_broadcast([P, TAIL, 128]), ALU.add))
            act.need(m)
            m = act.done(lambda e, ts=ts: e.activation(cx[:, ts, :], cx[:, ts, :], ACT.Tanh))
            adder.need(m, M["x_attn", 1, NT - 1])
            m = adder.done(lambda e, ts=ts: e.tensor_tensor(x[:, ts, :], cx[:, ts, :], x[:, ts, :], ALU.add))
            sp.need(m)
            sp.dma(lambda e, ts=ts: e.dma_start(o_v[:, ts, :], x[:, ts, :]), s_out)
            n_out += 16
        sp.need((s_out, n_out))

        block = ctx.enter_context(nc.Block())

        @block.tensor
        def _(e):
            pe.run(e)

        @block.vector
        def _(e):
            dve.run(e)

        @block.scalar
        def _(e):
            act.run(e)

        @block.gpsimd
        def _(e):
            pool.run(e)

        @block.sync
        def _(e):
            sp.run(e)


_INS = ["x", "ctx_1024", "L0_xattn_Wq", "L0_xattn_bq", "L0_xattn_Wk", "L0_xattn_bk", "L0_xattn_Wv", "L0_xattn_bv",
        "L0_xattn_Wo", "L0_xattn_bo", "L0_ffn_W_gate", "L0_ffn_b_gate", "L0_ffn_W1", "L0_ffn_b1", "L0_ffn_W2",
        "L0_ffn_b2", "L1_xattn_Wq", "L1_xattn_Wk", "L1_xattn_Wv", "L1_xattn_Wd", "L1_ffn_wf", "L1_ffn_uf",
        "L1_ffn_bf", "L1_ffn_wi", "L1_ffn_ui", "L1_ffn_bi", "L1_ffn_wc", "L1_ffn_uc", "L1_ffn_bc", "L1_ffn_wo",
        "L1_ffn_uo", "L1_ffn_bo", "L1_ffn_in_c"]


def constants():
    c = np.zeros((P, 160), np.float32)
    c[:, 0:128] = np.eye(128, dtype=np.float32)
    p = np.arange(P)
    c[p, 128 + (p % 64) // 8] = 1.0
    c[:, 136:144] = np.arange(8, dtype=np.float32)
    return c


def kernel(**inputs):
    import numpy as _np
    import concourse.bacc as _bacc
    from concourse import mybir as _mybir
    from concourse.bass_utils import run_bass_kernel_spmd as _run

    nc = _bacc.Bacc("TRN2", target_bir_lowering=False, num_devices=1)
    arrays, aps = {}, {}
    for name in _INS:
        v = _np.ascontiguousarray(inputs[name])
        arrays[f"in_{name}_dram"] = v
        aps[name] = nc.dram_tensor(f"in_{name}_dram", v.shape, _mybir.dt.from_np(v.dtype), kind="ExternalInput").ap()
    c = constants()
    arrays["constants_dram"] = c
    cap = nc.dram_tensor("constants_dram", c.shape, F32, kind="ExternalInput").ap()
    out = nc.dram_tensor("out_0_dram", (128, 64, 128), F32, kind="ExternalOutput").ap()
    build(nc, aps, cap, out)
    r = _run(nc, [arrays], core_ids=[0])
    return r.results[0]["out_0_dram"]
```

```python
from contextlib import ExitStack

import numpy as np

import concourse.bass as bass
from concourse import mybir

P = 128
NT = 64
H = 16
E = 8
EPS = 1e-5
SCALE = 1.0 / float(np.sqrt(8.0))
F32 = mybir.dt.float32
U32 = mybir.dt.uint32
ALU = mybir.AluOpType
ACT = mybir.ActivationFunctionType
AX = mybir.AxisListType

LOADS = [1, 1, 2, 4, 8, 8, 8, 8, 8, 8, 8]
TAIL = 8
SETUP = 1.5
PLACE = {
    "stat0": -0.0554,
    "scale0": 0.15,
    "ctx": 0.262,
    "turnx0": 1.9578,
    "kv0": 2.7886,
    "q0": 2.8136,
    "S0": 3.4136,
    "exp0": 3.5886,
    "e0": 4.3781,
    "v0": 5.4138,
    "o0": 6.6636,
    "a0": 7.8736,
    "p0": 8.0589,
    "scale1": 8.2136,
    "turnx1": 8.861,
    "gate": 9.8589,
    "hidden": 9.8839,
    "gtop": 9.9299,
    "gidx": 10.0089,
    "gw": 10.0839,
    "turnw": 11.3089,
    "experts": 11.3339,
    "scale2": 11.5839,
    "turnx2": 12.4674,
    "kv1": 13.4089,
    "q1": 13.4175,
    "S1": 14.1304,
    "exp1": 14.3839,
    "e1": 15.2339,
    "v1": 16.3589,
    "o1": 17.4839,
    "a1": 18.435,
    "p1": 19.6768,
    "scale3": 20.0552,
    "turnx3": 21.0647,
    "inputs": 21.6018,
    "stepA": 21.8018,
    "updA": 21.9268,
    "stepB": 22.3082,
    "updB": 22.3268,
}


class Queue:

    def __init__(self, sem):
        self.sem = sem
        self.count = 0
        self.seen = {}
        self.ops = []

    def op(self, fn):
        self.ops.append(fn)

    def done(self, fn):
        sem = self.sem
        self.count += 1
        self.ops.append(lambda e: fn(e).then_inc(sem, 1))
        return (sem, self.count)

    def dma(self, fn, sem):
        self.ops.append(lambda e: fn(e).then_inc(sem, 16))

    def need(self, *marks):
        for sem, value in marks:
            key = sem.name
            if self.seen.get(key, 0) < value:
                self.seen[key] = value
                self.ops.append(lambda e, s=sem, v=value: e.wait_ge(s, v))

    def run(self, e):
        for fn in self.ops:
            fn(e)


def build(nc, a, const, out):
    ctx = ExitStack()
    with ctx:
        def sb(name, shape, dt=F32):
            return ctx.enter_context(nc.sbuf_tensor(name, shape, dt))

        def sem(name):
            return ctx.enter_context(nc.semaphore(name))

        pe, dve, act, pool, sp = (Queue(sem(n)) for n in ("s_pe", "s_dve", "s_act", "s_pool", "s_sp"))

        x = sb("x", [P, NT, 128])
        cx = sb("cx", [P, NT, 128])
        cst = sb("cst", [P, 128 + 8 + 8 + 16])
        ident = cst[:, 0:128]
        hmask = cst[:, 128:136]
        iota = cst[:, 136:144]
        wst = sb("wst", [P, 13, 128])
        wT = sb("wT", [P, 13, 128])
        wq1 = sb("wq1", [P, 128])
        wk1 = sb("wk1", [P, 128])
        wv1 = sb("wv1", [P, 128])
        wg = sb("wg", [P, 8])
        w1 = sb("w1", [P, E, 128])
        w2 = sb("w2", [P, E, 128])
        b2 = sb("b2", [E, 128])
        col = sb("col", [P, 24])
        bo0 = sb("bo0", [P, 128])
        bo1 = sb("bo1", [P, 128])
        bg = sb("bg", [P, 8])
        xn = sb("xn", [P, 8, 128])
        st = sb("st", [P, 8, 6])
        mv = sb("mv", [P, 8, 2])
        ve = sb("ve", [P, 8, 1])
        rs = sb("rs", [P, 8, 1])
        xT = sb("xT", [P, 8, 128])
        qT = sb("qT", [P, 4, 128])
        kT = sb("kT", [P, 2, 128])
        Km = sb("Km", [P, 4, 8, 128])
        Vb = sb("Vb", [P, 8, 2, 8, 32])
        mx = sb("mx", [P, 4, 16])
        Ex = sb("Ex", [P, 4, 1024])
        ET = sb("ET", [P, 4, 8, 128])
        raw = sb("raw", [P, 4, 256])
        rd = sb("rd", [P, 4, 16])
        att = sb("att", [P, 4, 128])
        aT = sb("aT", [P, 4, 128])
        hT = sb("hT", [P, 2, E, 128])
        sc = sb("sc", [P, 2, 8])
        top = sb("top", [P, 2, 8])
        tix = sb("tix", [P, 2, 8], U32)
        tif = sb("tif", [P, 2, 2])
        wa = sb("wa", [P, 2, 8])
        wb = sb("wb", [P, 2, 8])
        we = sb("we", [P, 2, 8])
        weT = sb("weT", [E, 2, 128])
        acc = sb("acc", [P, 2, 2, 128])
        TG = sb("TG", [P, 2, 128])
        CG = sb("CG", [P, 3, 128])
        AB = sb("AB", [P, 2, 128])
        cU = sb("cU", [P, 128])

        banks = [ctx.enter_context(nc.psum_tensor(f"ps{i}", [P, 512], F32)) for i in range(8)]
        lstm = banks[7]
        ring = [[] for _ in range(7)]
        turn = [0]

        def bank():
            i = turn[0] % 7
            turn[0] += 1
            pe.need(*ring[i])
            ring[i] = []
            return i, banks[i]

        def free(i, mark):
            ring[i].append(mark)

        x_v = a["x"].rearrange("a b d -> (a b) d").rearrange("(t p) d -> p t d", p=P)
        c_v = a["ctx_1024"].rearrange("a b d -> (a b) d").rearrange("(t p) d -> p t d", p=P)
        o_v = out.rearrange("a b d -> (a b) d").rearrange("(t p) d -> p t d", p=P)
        x_in, c_in = {}, {}
        starts = np.cumsum([0] + LOADS)

        def load(q, name, fn):
            s = sem("l_" + name)
            q.dma(fn, s)
            return (s, 16)

        def load_x(c):
            t0, t1 = int(starts[c]), int(starts[c + 1])
            m = load(sp, f"x{c}", lambda e: e.dma_start(x[:, t0:t1, :], x_v[:, t0:t1, :]))
            for t in range(t0, t1):
                x_in[t] = m

        def load_c(c):
            t0, t1 = int(starts[c]), int(starts[c + 1])
            m = load(sp, f"c{c}", lambda e: e.dma_start(cx[:, t0:t1, :], c_v[:, t0:t1, :]))
            for t in range(t0, t1):
                c_in[t] = m

        def column(ap):
            return ap.rearrange("(n a) -> n a", a=1)

        def row(ap):
            return ap.rearrange("(a n) -> a n", a=1)

        W = {}
        in_const = load(act, "const", lambda e: e.dma_start(cst[:, :], const))
        load_x(0)
        load_c(0)
        squares = ["L0_xattn_Wq", "L0_xattn_Wk", "L0_xattn_Wv", "L0_xattn_Wo", "L1_xattn_Wd",
                   "L1_ffn_wf", "L1_ffn_wi", "L1_ffn_wc", "L1_ffn_uf", "L1_ffn_ui", "L1_ffn_uc",
                   "L1_ffn_wo", "L1_ffn_uo"]
        factor = {"L1_ffn_wf": 0.5, "L1_ffn_wi": 0.5, "L1_ffn_uf": 0.25, "L1_ffn_ui": 0.25,
                  "L1_ffn_uc": 0.5, "L1_ffn_uo": 0.5}

        def square(n):
            return load(act if n < 2 else sp, f"sq{n}", lambda e: e.dma_start(wst[:, n, :], a[squares[n]]))

        in_sq = [square(n) for n in range(4)]
        BQ, BK, BV, B1, BF, BI, BC, CI = 0, 1, 2, 3, 11, 12, 13, 14
        cols = {"L0_xattn_bq": BQ, "L0_xattn_bk": BK, "L0_xattn_bv": BV, "L1_ffn_bf": BF,
                "L1_ffn_bi": BI, "L1_ffn_bc": BC, "L1_ffn_in_c": CI}

        def load_col(name):
            c = cols[name]
            return load(pool, name, lambda e: e.dma_start(col[:, c:c + 1], column(a[name])))

        in_col = {n: load_col(n) for n in ("L0_xattn_bq", "L0_xattn_bk", "L0_xattn_bv")}
        in_bo0 = load(pool, "bo0", lambda e: e.dma_start(bo0[:, :], row(a["L0_xattn_bo"]).to_broadcast([P, 128])))
        load_x(1)
        load_c(1)
        load_x(2)
        load_c(2)
        for c in range(3, 5):
            load_x(c)
            load_c(c)

        def heads(name, tile):
            return load(sp, name, lambda e: e.dma_start(tile[:, :].rearrange("d (h k) -> d h k", h=H),
                                                        a[name].rearrange("h d k -> d h k")))

        in_k1 = heads("L1_xattn_Wk", wk1)
        in_v1 = heads("L1_xattn_Wv", wv1)
        in_wg = load(pool, "wg", lambda e: e.dma_start(wg[:, :], a["L0_ffn_W_gate"]))
        in_bg = load(pool, "bg", lambda e: e.dma_start(bg[:, :], row(a["L0_ffn_b_gate"]).to_broadcast([P, 8])))
        in_w1 = load(sp, "w1", lambda e: e.dma_start(w1[:, :, :], a["L0_ffn_W1"].rearrange("e d h -> d e h")))
        in_b1 = load(pool, "b1", lambda e: e.dma_start(col[:, B1:B1 + E], a["L0_ffn_b1"].rearrange("e h -> h e"),
                                                                 allow_slow_non_contiguous=True))
        in_w2 = load(sp, "w2", lambda e: e.dma_start(w2[:, :, :], a["L0_ffn_W2"].rearrange("e d h -> d e h")))
        in_b2 = load(pool, "b2", lambda e: e.dma_start(b2[:, :], a["L0_ffn_b2"]))
        in_q1 = heads("L1_xattn_Wq", wq1)
        in_sq += [square(n) for n in range(4, 13)]
        for n in ("L1_ffn_bf", "L1_ffn_bi", "L1_ffn_bc", "L1_ffn_in_c"):
            in_col[n] = load_col(n)
        in_bo1 = load(pool, "bo1", lambda e: e.dma_start(bo1[:, :], row(a["L1_ffn_bo"]).to_broadcast([P, 128])))
        for c in range(5, len(LOADS)):
            load_x(c)
            load_c(c)

        z = pool.done(lambda e: e.memset(Vb[:, :, :, :, :], 0.0))
        pool.need(z)
        z = pool.done(lambda e: e.memset(Vb[0:64, :, :, :, 16:17], 1.0))
        pool.need(z)
        vb_set = pool.done(lambda e: e.memset(Vb[64:128, :, :, :, 17:18], 1.0))
        half = sb("half", [P, 1])
        pool.need(vb_set)
        half_set = pool.done(lambda e: e.memset(half[:, :], -0.5))

        w_ready = {}

        def turn_weight(n):
            i, b = bank()
            pe.need(in_const, in_sq[n])
            m = pe.done(lambda e: e.transpose(b[:, 0:128], wst[:, n, :], ident))
            act.need(m)
            f = factor.get(squares[n], 1.0)
            m = act.done(lambda e: e.activation(wT[:, n, :], b[:, 0:128], ACT.Copy, scale=f))
            free(i, m)
            w_ready[n] = m

        WQ, WK, WV, WO, WD, WF, WI, WC, UF, UI, UC, WX, UO = range(13)

        M = {}

        def ctx_turn(t):
            i, b = bank()
            pe.need(in_const, c_in[t])
            m = pe.done(lambda e: e.transpose(b[:, 0:128], cx[:, t, :], ident))
            act.need(m)
            M["cT", t] = act.done(lambda e: e.activation(cx[:, t, :], b[:, 0:128], ACT.Copy))
            free(i, M["cT", t])

        def keys_values(L, t):
            i, b = bank()
            wk, wv = (wT[:, WK, :], wT[:, WV, :]) if L == 0 else (wk1[:, :], wv1[:, :])
            pe.need(M["cT", t])
            pe.need(*((w_ready[WK], w_ready[WV]) if L == 0 else (in_k1, in_v1)))
            k = pe.done(lambda e: e.matmul(b[:, 0:128], wk, cx[:, t, :], start=True, stop=True))
            wv2 = wv.rearrange("p (n two d) -> p two n d", two=2, d=8)
            for s in range(2):
                for h in range(2):
                    fn = (lambda e, s=s, h=h: e.matmul(b[64 * h:64 * h + 64, 128 + 64 * s:192 + 64 * s],
                                                       cx[:, t, 64 * s:64 * s + 64], wv2[:, h, :, :],
                                                       start=True, stop=True, skip_group_check=True))
                    if (s, h) == (1, 1):
                        v = pe.done(fn)
                    else:
                        pe.op(fn)
            vs = 4 * L + t % 4
            act.need(v)
            act.need(vb_set)
            if t >= 4:
                act.need(M["pv", L, t - 4])
            for h in range(2):
                src = b[64 * h:64 * h + 64, 128:256].rearrange("p (s n d) -> p s n d", s=2, d=8)
                dst = Vb[64 * h:64 * h + 64, vs, :, :, 8 * h:8 * h + 8]
                m = act.done(lambda e, src=src, dst=dst: e.activation(dst, src, ACT.Copy))
            M["V", L, t] = m
            if t >= 1:
                act.need(M["K", L, t - 1])
            if L == 0:
                act.need(in_col["L0_xattn_bk"])
                m = act.done(lambda e: e.activation(kT[:, L, :], b[:, 0:128], ACT.Identity,
                                                    bias=col[:, BK:BK + 1]))
            else:
                m = act.done(lambda e: e.activation(kT[:, L, :], b[:, 0:128], ACT.Copy))
            free(i, m)
            pool.need(in_const, m)
            if t >= 2:
                pool.need(M["S", L, t - 2])
            M["K", L, t] = pool.done(lambda e: e.tensor_tensor(
                Km[:, 2 * L + t % 2, :, :], kT[:, L, :].unsqueeze(1).to_broadcast([P, 8, 128]),
                hmask.unsqueeze(2).to_broadcast([P, 8, 128]), ALU.mult))

        def norm(k, t, src):
            s = 2 * k + t % 2
            dve.need(*src)
            m = dve.done(lambda e: e.bn_stats(st[:, s, :], x[:, t, :]))
            dve.need(m)
            m = dve.done(lambda e: e.bn_aggr(mv[:, s, :], st[:, s, :]))
            dve.need(m)
            if t >= 2:
                dve.need(M["rs", k, t - 2])
            m = dve.done(lambda e: e.tensor_scalar(ve[:, s, :], mv[:, s, 1:2], EPS, None, ALU.add))
            pool.need(m, half_set)
            if t >= 2:
                pool.need(M["n", k, t - 2])
            M["rs", k, t] = pool.done(lambda e: e.tensor_tensor(rs[:, s, :], ve[:, s, :], half[:, :], ALU.pow))

        def scale(k, t):
            s = 2 * k + t % 2
            dve.need(M["rs", k, t])
            if t >= 2:
                dve.need(M["xn_read", k, t - 2])
            M["n", k, t] = dve.done(lambda e: e.tensor_scalar(xn[:, s, :], x[:, t, :], mv[:, s, 0:1], rs[:, s, :],
                                                              ALU.subtract, ALU.mult))
            if k == 0:
                pool.need(in_bo0)
                pool.need(M["n", 0, t])
                M["xb", t] = pool.done(lambda e: e.tensor_tensor(x[:, t, :], x[:, t, :], bo0[:, :], ALU.add))

        def turn_x(t, k):
            s = 2 * k + t % 2
            i, b = bank()
            pe.need(M["n", k, t])
            m = pe.done(lambda e: e.transpose(b[:, 0:128], xn[:, s, :], ident))
            M["xn_read", k, t] = m
            act.need(m)
            if t >= 2:
                act.need(M["xT_read", k, t - 2])
            m = act.done(lambda e: e.activation(xT[:, s, :], b[:, 0:128], ACT.Copy))
            free(i, m)
            M["xT", k, t] = m

        def query(L, t):
            s = t % 2
            i, b = bank()
            pe.need(M["xT", 2 * L, t])
            pe.need(w_ready[WQ] if L == 0 else in_q1)
            w = wT[:, WQ, :] if L == 0 else wq1[:, :]
            m = pe.done(lambda e: e.matmul(b[:, 0:128], w, xT[:, 4 * L + s, :], start=True, stop=True))
            M["xT_read", 2 * L, t] = m
            act.need(m)
            if t >= 2:
                act.need(M["S", L, t - 2])
            if L == 0:
                act.need(in_col["L0_xattn_bq"])
                m = act.done(lambda e: e.activation(qT[:, s, :], b[:, 0:128], ACT.Identity,
                                                    bias=col[:, BQ:BQ + 1]))
            else:
                m = act.done(lambda e: e.activation(qT[:, 2 + s, :], b[:, 0:128], ACT.Copy))
            free(i, m)
            M["q", L, t] = m

        def scores(L, t):
            s = 2 * L + t % 2
            pe.need(M["q", L, t], M["K", L, t])
            (i0, b0), (i1, b1) = bank(), bank()
            marks = []
            for r, b in ((0, b0), (1, b1)):
                for n in range(2):
                    fn = (lambda e, r=r, b=b, n=n: e.matmul(
                        b[64 * n:64 * n + 64, :].rearrange("p (j k) -> p j k", j=8),
                        qT[64 * r:64 * r + 64, s, 64 * n:64 * n + 64],
                        Km[64 * r:64 * r + 64, s, :, 64 * n:64 * n + 64],
                        start=True, stop=True, skip_group_check=True))
                    if n:
                        marks.append(pe.done(fn))
                    else:
                        pe.op(fn)
            M["S", L, t] = marks[1]
            if t >= 2:
                dve.need(M["ET_mm", L, t - 2])
            for r, (i, b) in enumerate(((i0, b0), (i1, b1))):
                S = b[:, :].rearrange("p (j k) -> p j k", j=8)
                mr = mx[:, s, 8 * r:8 * r + 8]
                Er = Ex[:, s, 512 * r:512 * r + 512]
                dve.need(marks[r])
                m = dve.done(lambda e, S=S, mr=mr: e.tensor_reduce(mr, S, AX.X, ALU.max))
                dve.need(m)
                m = dve.done(lambda e, S=S, mr=mr, Er=Er: e.tensor_tensor(
                    Er.rearrange("p (j k) -> p j k", j=8), S,
                    mr.unsqueeze(2).to_broadcast([P, 8, 64]), ALU.subtract))
                free(i, m)
                M["D%d" % r, L, t] = m

        def exps(L, t):
            s = 2 * L + t % 2
            for r in range(2):
                Er = Ex[:, s, 512 * r:512 * r + 512]
                act.need(M["D%d" % r, L, t])
                M["E%d" % r, L, t] = act.done(lambda e, Er=Er: e.activation(Er, Er, ACT.Exp, scale=SCALE))

        def turn_e(L, t):
            s = 2 * L + t % 2
            for r in range(2):
                i, b = bank()
                pe.need(M["E%d" % r, L, t])
                for n in range(4):
                    g = 4 * r + n
                    fn = (lambda e, n=n, g=g, b=b: e.transpose(b[:, 128 * n:128 * n + 128],
                                                               Ex[:, s, 128 * g:128 * g + 128], ident))
                    if n == 3:
                        m = pe.done(fn)
                    else:
                        pe.op(fn)
                act.need(m)
                if t >= 2:
                    act.need(M["pv", L, t - 2])
                M["ET%d" % r, L, t] = act.done(lambda e, b=b, r=r: e.activation(
                    ET[:, s, 4 * r:4 * r + 4, :], b[:, :].rearrange("p (n q) -> p n q", n=4), ACT.Copy))
                free(i, M["ET%d" % r, L, t])
            M["ET_mm", L, t] = m

        def values(L, t):
            s = 2 * L + t % 2
            vs = 4 * L + t % 4
            i, b = bank()
            pe.need(M["ET0", L, t], M["ET1", L, t], M["V", L, t])
            for n in range(2):
                for g in range(8):
                    j, c = g % 4, g // 4
                    fn = (lambda e, n=n, g=g, j=j, c=c: e.matmul(
                        b[32 * j:32 * j + 32, 128 * c + 64 * n:128 * c + 64 * n + 64],
                        Vb[:, vs, n, g, :], ET[:, s, g, 64 * n:64 * n + 64],
                        start=True, stop=True, skip_group_check=True))
                    if (n, g) == (1, 7):
                        m = pe.done(fn)
                    else:
                        pe.op(fn)
            M["pv", L, t] = m
            act.need(m)
            if t >= 2:
                act.need(M["raw_mm", L, t - 2])
            M["raw", L, t] = act.done(lambda e: e.activation(raw[:, s, :], b[:, 0:256], ACT.Copy))
            free(i, M["raw", L, t])

        def turn_o(L, t):
            s = 2 * L + t % 2
            i, b = bank()
            pe.need(M["raw", L, t])
            pe.op(lambda e: e.transpose(b[:, 0:128], raw[:, s, 0:128], ident))
            m = pe.done(lambda e: e.transpose(b[:, 128:256], raw[:, s, 128:256], ident))
            M["raw_mm", L, t] = m
            o = b[:, 0:256].rearrange("p (g r) -> p g r", r=32)
            dve.need(m)
            m = dve.done(lambda e: e.reciprocal(rd[:, s, :].rearrange("p (g two) -> p g two", two=2),
                                                o[:, :, 16:18]))
            dve.need(m)
            if t >= 2:
                dve.need(M["att_mm", L, t - 2])
            M["att", L, t] = dve.done(lambda e: e.tensor_tensor(
                att[:, s, :].rearrange("p (g two d) -> p g two d", two=2, d=8),
                o[:, :, 0:16].rearrange("p g (two d) -> p g two d", two=2),
                rd[:, s, :].rearrange("p (g two) -> p g two", two=2).unsqueeze(3).to_broadcast([P, 8, 2, 8]),
                ALU.mult))
            free(i, M["att", L, t])

        def turn_a(L, t):
            s = 2 * L + t % 2
            i, b = bank()
            pe.need(M["att", L, t])
            m = pe.done(lambda e: e.transpose(b[:, 0:128], att[:, s, :], ident))
            M["att_mm", L, t] = m
            act.need(m)
            if t >= 2:
                act.need(M["o_mm", L, t - 2])
            if L == 0:
                act.need(in_col["L0_xattn_bv"])
                m = act.done(lambda e: e.activation(aT[:, s, :], b[:, 0:128], ACT.Identity,
                                                    bias=col[:, BV:BV + 1]))
            else:
                m = act.done(lambda e: e.activation(aT[:, s, :], b[:, 0:128], ACT.Copy))
            free(i, m)
            M["aT", L, t] = m

        def project(L, t):
            s = 2 * L + t % 2
            n = WO if L == 0 else WD
            i, b = bank()
            pe.need(M["aT", L, t], w_ready[n])
            m = pe.done(lambda e: e.matmul(b[:, 0:128], aT[:, s, :], wT[:, n, :], start=True, stop=True))
            M["o_mm", L, t] = m
            dve.need(m)
            if L == 0:
                dve.need(M["xb", t])
            m = dve.done(lambda e: e.tensor_tensor(x[:, t, :], b[:, 0:128], x[:, t, :], ALU.add))
            free(i, m)
            M["x_attn", L, t] = m
            norm(1 + 2 * L, t, [m])

        def start_x(t):
            norm(0, t, [x_in[t]])

        def gate(t):
            s = t % 2
            i, b = bank()
            pe.need(M["xT", 1, t], in_wg)
            m = pe.done(lambda e: e.matmul(b[:, 0:8], xT[:, 2 + s, :], wg[:, :], start=True, stop=True))
            dve.need(m, in_bg)
            m = dve.done(lambda e: e.tensor_tensor(sc[:, s, :], b[:, 0:8], bg[:, :], ALU.add))
            free(i, m)
            M["sc", t] = m

        def gate_top(t):
            s = t % 2
            dve.need(M["sc", t])
            m = dve.done(lambda e: e.max(top[:, s, :], sc[:, s, :]))
            dve.need(m)
            m = dve.done(lambda e: e.max_index(tix[:, s, :], top[:, s, :], sc[:, s, :]))
            M["tix", t] = m

        def gate_index(t):
            s = t % 2
            dve.need(M["tix", t])
            M["tif", t] = dve.done(lambda e: e.tensor_copy(tif[:, s, :], tix[:, s, 0:2]))

        def gate_weights(t):
            s = t % 2
            dve.need(M["tif", t], in_const)
            m = dve.done(lambda e: e.tensor_scalar(wa[:, s, :], iota, tif[:, s, 0:1], top[:, s, 0:1],
                                                   ALU.is_equal, ALU.mult))
            m = dve.done(lambda e: e.tensor_scalar(wb[:, s, :], iota, tif[:, s, 1:2], top[:, s, 1:2],
                                                   ALU.is_equal, ALU.mult))
            dve.need(m)
            if t >= 2:
                dve.need(M["we_mm", t - 2])
            M["we", t] = dve.done(lambda e: e.tensor_tensor(we[:, s, :], wa[:, s, :], wb[:, s, :], ALU.add))

        def hidden(t):
            s = t % 2
            pe.need(M["xT", 1, t], in_w1)
            act.need(in_b1)
            for c in range(2):
                i, b = bank()
                for n in range(4):
                    fn = (lambda e, b=b, c=c, n=n: e.matmul(b[:, 128 * n:128 * n + 128], w1[:, 4 * c + n, :],
                                                            xT[:, 2 + s, :], start=True, stop=True,
                                                            skip_group_check=True))
                    if n == 3:
                        m = pe.done(fn)
                    else:
                        pe.op(fn)
                act.need(m)
                if t >= 2:
                    act.need(M["y_mm%d" % c, t - 2])
                for n in range(4):
                    k = 4 * c + n
                    fn = (lambda e, b=b, n=n, k=k: e.activation(hT[:, s, k, :], b[:, 128 * n:128 * n + 128],
                                                                ACT.Relu, bias=col[:, B1 + k:B1 + k + 1]))
                    if n == 3:
                        M["h%d" % c, t] = act.done(fn)
                    else:
                        act.op(fn)
                free(i, M["h%d" % c, t])
            M["xT_read", 1, t] = m

        def turn_w(t):
            s = t % 2
            i, b = bank()
            pe.need(M["we", t])
            m = pe.done(lambda e: e.transpose(b[0:8, 0:128], we[:, s, :], ident))
            M["we_mm", t] = m
            act.need(m)
            if t >= 2:
                act.need(M["b2_mm", t - 2])
            M["weT", t] = act.done(lambda e: e.activation(weT[:, s, :], b[0:8, 0:128], ACT.Copy))
            free(i, M["weT", t])

        def experts(t):
            s = t % 2
            held = []
            for c in range(2):
                i, b = bank()
                pe.need(M["h%d" % c, t], in_w2)
                for n in range(4):
                    k = 4 * c + n
                    fn = (lambda e, b=b, k=k, n=n: e.matmul(b[:, 128 * n:128 * n + 128], hT[:, s, k, :],
                                                            w2[:, k, :], start=True, stop=True,
                                                            skip_group_check=True))
                    if n == 3:
                        m = pe.done(fn)
                    else:
                        pe.op(fn)
                M["y_mm%d" % c, t] = m
                held.append((i, b, m))
            i2, bb = bank()
            pe.need(M["weT", t], in_b2)
            mb = pe.done(lambda e: e.matmul(bb[:, 0:128], weT[:, s, :], b2[:, :], start=True, stop=True))
            M["b2_mm", t] = mb
            last = [None, None]
            for n in range(4):
                for c in range(2):
                    i, b, m = held[c]
                    dve.need(m)
                    k = 4 * c + n
                    y = b[:, 128 * n:128 * n + 128]
                    w = we[:, s, k:k + 1]
                    d = acc[:, s, c, :]
                    if n == 0 and c == 1:
                        last[1] = dve.done(lambda e, y=y, w=w, d=d: e.tensor_scalar(d, y, w, None, ALU.mult))
                        continue
                    src = x[:, t, :] if n == 0 else d
                    if n:
                        dve.need(last[c])
                    last[c] = dve.done(lambda e, y=y, w=w, d=d, src=src: e.scalar_tensor_tensor(
                        d, y, w, src, ALU.mult, ALU.add))
            for c in range(2):
                free(held[c][0], last[c])
            dve.need(mb, last[1])
            m = dve.done(lambda e: e.tensor_tensor(acc[:, s, 1, :], bb[:, 0:128], acc[:, s, 1, :], ALU.add))
            free(i2, m)
            dve.need(m)
            m = dve.done(lambda e: e.tensor_tensor(x[:, t, :], acc[:, s, 0, :], acc[:, s, 1, :], ALU.add))
            M["x_moe", t] = m
            norm(2, t, [m])

        def inputs(t):
            s = t % 2
            i, b = bank()
            pe.need(M["xT", 3, t], w_ready[WX], w_ready[WF], w_ready[WI], w_ready[WC])
            m = pe.done(lambda e: e.matmul(b[:, 0:128], xT[:, 6 + s, :], wT[:, WX, :], start=True, stop=True))
            act.need(m)
            act.need(M["V", 1, t])
            M["xo", t] = act.done(lambda e: e.activation(cx[:, t, :], b[:, 0:128], ACT.Copy))
            free(i, M["xo", t])
            if t:
                pe.need(M["gates", 2 * t - 1])
            for n, w in enumerate((WF, WI, WC)):
                fn = (lambda e, n=n, w=w: e.matmul(lstm[:, 128 * n:128 * n + 128], wT[:, w, :], xT[:, 6 + s, :],
                                                   start=(n == 0), stop=False, skip_group_check=True))
                if n == 2:
                    M["xT_read", 3, t] = pe.done(fn)
                else:
                    pe.op(fn)

        def step(k):
            t, o = k // 2, 64 * (k % 2)
            pe.need(M["C", k - 1], w_ready[UF], w_ready[UI], w_ready[UC])
            c_in_now = CG[:, k % 3, 0:64]
            for n, w in enumerate((UF, UI, UC)):
                fn = (lambda e, n=n, w=w: e.matmul(lstm[:, 128 * n + o:128 * n + o + 64], wT[:, w, :], c_in_now,
                                                   start=False, stop=True, skip_group_check=True))
                if n == 2:
                    m = pe.done(fn)
                else:
                    pe.op(fn)
            act.need(m)
            if k >= 2:
                act.need(M["AB", k - 2])
            act.need(cols_half, in_col["L1_ffn_bc"])
            if k >= 3:
                act.need(M["AB", k - 3])
            act.op(lambda e: e.activation(TG[:, k % 2, 0:64], lstm[:, o:o + 64], ACT.Tanh, bias=col[:, BF + 4:BF + 5]))
            act.op(lambda e: e.activation(TG[:, k % 2, 64:128], lstm[:, 128 + o:192 + o], ACT.Tanh,
                                          bias=col[:, BF + 5:BF + 6]))
            M["gates", k] = act.done(lambda e: e.activation(CG[:, k % 3, 64:128], lstm[:, 256 + o:320 + o],
                                                            ACT.Tanh, bias=col[:, BC:BC + 1]))

        def update(k):
            dve.need(M["gates", k], M["C", k - 1])
            M["AB", k] = dve.done(lambda e: e.scalar_tensor_tensor(AB[:, k % 2, :], TG[:, k % 2, :], 1.0,
                                                                   CG[:, k % 3, :], ALU.add, ALU.mult))
            dve.need(M["AB", k])
            M["C", k] = dve.done(lambda e: e.scalar_tensor_tensor(CG[:, (k + 1) % 3, 0:64], AB[:, k % 2, 0:64], 0.5,
                                                                  AB[:, k % 2, 64:128], ALU.mult, ALU.add))

        for n in (WQ, WK, WV, WO):
            turn_weight(n)

        stages = {
            "stepA": lambda t: step(2 * t),
            "ctx": lambda t: ctx_turn(t),
            "stat0": lambda t: start_x(t),
            "scale0": lambda t: scale(0, t),
            "kv0": lambda t: keys_values(0, t),
            "turnx0": lambda t: turn_x(t, 0),
            "q0": lambda t: query(0, t),
            "turnw": lambda t: turn_w(t),
            "experts": lambda t: experts(t),
            "updA": lambda t: update(2 * t),
            "S0": lambda t: scores(0, t),
            "S1": lambda t: scores(1, t),
            "exp0": lambda t: exps(0, t),
            "exp1": lambda t: exps(1, t),
            "e0": lambda t: turn_e(0, t),
            "e1": lambda t: turn_e(1, t),
            "v0": lambda t: values(0, t),
            "v1": lambda t: values(1, t),
            "gate": lambda t: gate(t),
            "gtop": lambda t: gate_top(t),
            "gidx": lambda t: gate_index(t),
            "gw": lambda t: gate_weights(t),
            "hidden": lambda t: hidden(t),
            "o0": lambda t: turn_o(0, t),
            "o1": lambda t: turn_o(1, t),
            "a0": lambda t: turn_a(0, t),
            "a1": lambda t: turn_a(1, t),
            "p0": lambda t: project(0, t),
            "p1": lambda t: project(1, t),
            "stepB": lambda t: step(2 * t + 1),
            "turnx1": lambda t: turn_x(t, 1),
            "turnx2": lambda t: turn_x(t, 2),
            "turnx3": lambda t: turn_x(t, 3),
            "kv1": lambda t: keys_values(1, t),
            "q1": lambda t: query(1, t),
            "inputs": lambda t: inputs(t),
            "scale1": lambda t: scale(1, t),
            "scale2": lambda t: scale(2, t),
            "scale3": lambda t: scale(3, t),
            "updB": lambda t: update(2 * t + 1),
        }

        cols_half = None

        def recurrent_setup():
            act.need(in_col["L1_ffn_bf"], in_col["L1_ffn_bi"], in_col["L1_ffn_in_c"])
            m = act.done(lambda e: e.activation(col[:, BF + 4:BF + 6], col[:, BF:BF + 2], ACT.Copy, scale=0.5))
            M["C", -1] = act.done(lambda e: e.activation(CG[:, 0, 0:64], col[:, CI:CI + 1].to_broadcast([P, 64]),
                                                         ACT.Copy, scale=2.0))
            return m

        turns = sorted((t + p, n, t) for n, p in PLACE.items() for t in range(NT))
        setup = [lambda n=n: turn_weight(n) for n in range(4, 13)] + [recurrent_setup]
        for at, n, t in turns:
            while setup and at >= SETUP + 0.15 * (10 - len(setup)):
                m = setup.pop(0)()
                cols_half = m or cols_half
            stages[n](t)

        i, b = bank()
        K = 2 * NT - 1
        pe.need(M["C", K], w_ready[UO])
        pe.op(lambda e: e.matmul(b[0:64, 0:128], CG[:, (K + 1) % 3, 0:64], wT[:, UO, :], start=True, stop=True))
        m = pe.done(lambda e: e.matmul(b[64:128, 0:128], CG[:, (K + 1) % 3, 0:64], wT[:, UO, :],
                                       start=True, stop=True, skip_group_check=True))
        dve.need(m, in_bo1)
        cu = dve.done(lambda e: e.tensor_tensor(cU[:, :], b[:, 0:128], bo1[:, :], ALU.add))
        s_out = sem("s_out")
        n_out = 0
        for c in range(NT // TAIL):
            ts = slice(TAIL * c, TAIL * c + TAIL)
            adder = pool if c % 4 == 3 else dve
            adder.need(cu, M["xo", NT - 1])
            m = adder.done(lambda e, ts=ts: e.tensor_tensor(
                cx[:, ts, :], cx[:, ts, :], cU[:, :].unsqueeze(1).to_broadcast([P, TAIL, 128]), ALU.add))
            act.need(m)
            m = act.done(lambda e, ts=ts: e.activation(cx[:, ts, :], cx[:, ts, :], ACT.Tanh))
            adder.need(m, M["x_attn", 1, NT - 1])
            m = adder.done(lambda e, ts=ts: e.tensor_tensor(x[:, ts, :], cx[:, ts, :], x[:, ts, :], ALU.add))
            sp.need(m)
            sp.dma(lambda e, ts=ts: e.dma_start(o_v[:, ts, :], x[:, ts, :]), s_out)
            n_out += 16
        sp.need((s_out, n_out))

        block = ctx.enter_context(nc.Block())

        @block.tensor
        def _(e):
            pe.run(e)

        @block.vector
        def _(e):
            dve.run(e)

        @block.scalar
        def _(e):
            act.run(e)

        @block.gpsimd
        def _(e):
            pool.run(e)

        @block.sync
        def _(e):
            sp.run(e)


_INS = ["x", "ctx_1024", "L0_xattn_Wq", "L0_xattn_bq", "L0_xattn_Wk", "L0_xattn_bk", "L0_xattn_Wv", "L0_xattn_bv",
        "L0_xattn_Wo", "L0_xattn_bo", "L0_ffn_W_gate", "L0_ffn_b_gate", "L0_ffn_W1", "L0_ffn_b1", "L0_ffn_W2",
        "L0_ffn_b2", "L1_xattn_Wq", "L1_xattn_Wk", "L1_xattn_Wv", "L1_xattn_Wd", "L1_ffn_wf", "L1_ffn_uf",
        "L1_ffn_bf", "L1_ffn_wi", "L1_ffn_ui", "L1_ffn_bi", "L1_ffn_wc", "L1_ffn_uc", "L1_ffn_bc", "L1_ffn_wo",
        "L1_ffn_uo", "L1_ffn_bo", "L1_ffn_in_c"]


def constants():
    c = np.zeros((P, 160), np.float32)
    c[:, 0:128] = np.eye(128, dtype=np.float32)
    p = np.arange(P)
    c[p, 128 + (p % 64) // 8] = 1.0
    c[:, 136:144] = np.arange(8, dtype=np.float32)
    return c


def kernel(**inputs):
    import numpy as _np
    import concourse.bacc as _bacc
    from concourse import mybir as _mybir
    from concourse.bass_utils import run_bass_kernel_spmd as _run

    nc = _bacc.Bacc("TRN2", target_bir_lowering=False, num_devices=1)
    arrays, aps = {}, {}
    for name in _INS:
        v = _np.ascontiguousarray(inputs[name])
        arrays[f"in_{name}_dram"] = v
        aps[name] = nc.dram_tensor(f"in_{name}_dram", v.shape, _mybir.dt.from_np(v.dtype), kind="ExternalInput").ap()
    c = constants()
    arrays["constants_dram"] = c
    cap = nc.dram_tensor("constants_dram", c.shape, F32, kind="ExternalInput").ap()
    out = nc.dram_tensor("out_0_dram", (128, 64, 128), F32, kind="ExternalOutput").ap()
    build(nc, aps, cap, out)
    r = _run(nc, [arrays], core_ids=[0])
    return r.results[0]["out_0_dram"]
```

```python
from contextlib import ExitStack

import numpy as np

import concourse.bass as bass
from concourse import mybir

P = 128
NT = 64
H = 16
E = 8
EPS = 1e-5
SCALE = 1.0 / float(np.sqrt(8.0))
F32 = mybir.dt.float32
BF16 = mybir.dt.bfloat16
U32 = mybir.dt.uint32
ALU = mybir.AluOpType
ACT = mybir.ActivationFunctionType
AX = mybir.AxisListType

LOADS = [1, 1, 2, 4, 8, 8, 8, 8, 8, 8, 8]
AHEAD = 16
PIECES = 72
TAIL = [("dve", 4), ("pool", 4), ("dve", 8), ("pool", 8), ("dve", 8), ("dve", 8), ("pool", 8), ("dve", 8), ("dve", 8)]
DEPTH = 1
DIRECT = ()
SUM_ON_POOL = False
ON_POOL = (0, 1, 2, 3)
SETUP = 2.0
PLACE = {
    'st0': -0.4448,
    'ctx': -0.2363,
    'sp0': -0.1466,
    'scale0': 0.6,
    'turnx0': 1.1131,
    'q0': 1.9639,
    'kv0': 1.9857,
    'kv1': 2.2113,
    'xb': 2.8,
    'S0': 3.0875,
    'd00': 3.0891,
    'd01': 3.0907,
    'x00': 3.1872,
    's00': 3.2931,
    'x01': 3.3036,
    's01': 3.5891,
    'e00': 3.6597,
    'e01': 3.6853,
    'i0': 3.7091,
    'w0': 3.9018,
    'rt0': 4.2682,
    'v0': 4.5481,
    'n0': 4.5501,
    'p0': 5.122,
    'st1': 5.1962,
    'sp1': 5.2983,
    'scale1': 5.2997,
    'turnx1': 5.9968,
    'gate': 6.6725,
    'gtop': 6.7527,
    'h0': 7.7385,
    'r0': 7.7405,
    'h1': 7.7425,
    'r1': 7.818,
    'gidx': 7.8635,
    'gw': 7.9288,
    'gp': 7.9388,
    'turnw': 8.4243,
    'yb': 9.1094,
    'y0': 9.1788,
    'y1': 9.1808,
    'c0': 9.1848,
    'c1': 9.1868,
    'st2': 9.1888,
    'sp2': 9.2522,
    'scale2': 9.3136,
    'turnx2': 10.3647,
    'km1': 11.0474,
    'q1': 11.1995,
    'S1': 11.9685,
    'd10': 11.9773,
    'd11': 11.9793,
    'x10': 12.2386,
    'x11': 12.4031,
    's10': 12.5788,
    'e11': 12.8247,
    's11': 12.9166,
    'i1': 12.9698,
    'vm1': 13.1641,
    'w1': 13.1964,
    'e10': 13.2402,
    'rt1': 13.8951,
    'v1': 14.4651,
    'n1': 14.5093,
    'p1': 15.1997,
    'st3': 15.4172,
    'sp3': 15.4858,
    'scale3': 15.5781,
    'turnx3': 16.5876,
    'inputs': 17.1852,
    'stepA': 17.1949,
    'gA': 17.1999,
    'updA': 17.2049,
    'stepB': 17.6249,
    'gB': 17.6299,
    'updB': 17.6349,
}


class Queue:

    def __init__(self, sem):
        self.sem = sem
        self.count = 0
        self.seen = {}
        self.ops = []

    def op(self, fn):
        self.ops.append(fn)

    def done(self, fn):
        sem = self.sem
        self.count += 1
        self.ops.append(lambda e: fn(e).then_inc(sem, 1))
        return (sem, self.count)

    def dma(self, fn, sem):
        self.ops.append(lambda e: fn(e).then_inc(sem, 16))

    def need(self, *marks):
        for sem, value in marks:
            key = sem.name
            if self.seen.get(key, 0) < value:
                self.seen[key] = value
                self.ops.append(lambda e, s=sem, v=value: e.wait_ge(s, v))

    def run(self, e):
        for fn in self.ops:
            fn(e)


def build(nc, a, const, out):
    ctx = ExitStack()
    with ctx:
        def sb(name, shape, dt=F32):
            return ctx.enter_context(nc.sbuf_tensor(name, shape, dt))

        def sem(name):
            return ctx.enter_context(nc.semaphore(name))

        pe, dve, act, pool, sp = (Queue(sem(n)) for n in ("s_pe", "s_dve", "s_act", "s_pool", "s_sp"))

        x = sb("x", [P, NT, 128])
        cx = sb("cx", [P, NT, 128])
        cst = sb("cst", [P, 128 + 8 + 8 + 5])
        ident = cst[:, 0:128]
        hmask = cst[:, 128:136]
        iota = cst[:, 136:144]
        piece = cst[:, 144:147]
        side = cst[:, 147:149]
        wst = sb("wst", [P, 13, 128])
        wT = sb("wT", [P, 13, 128])
        wq1 = sb("wq1", [P, 128])
        wk1 = sb("wk1", [P, 128])
        wv1 = sb("wv1", [P, 128])
        wg = sb("wg", [P, 8])
        w1 = sb("w1", [P, E, 128])
        w2 = sb("w2", [P, E, 128])
        b2 = sb("b2", [PIECES, 128])
        b2p = sb("b2p", [PIECES, 3, 128], BF16)
        b2s = sb("b2s", [PIECES, 128], BF16)
        identb = sb("identb", [P, 128], BF16)
        col = sb("col", [P, 24])
        bo0 = sb("bo0", [P, 128])
        bo1 = sb("bo1", [P, 128])
        bg = sb("bg", [P, 8])
        xn = sb("xn", [P, 8, 128])
        st = sb("st", [P, 8, 6])
        mv = sb("mv", [P, 8, 2])
        ve = sb("ve", [P, 8, 1])
        rs = sb("rs", [P, 8, 1])
        xT = sb("xT", [P, 8, 128])
        qT = sb("qT", [P, 4, 128])
        kT = sb("kT", [P, 2, 128])
        kv1 = sb("kv1", [P, AHEAD, 256])
        Km = sb("Km", [P, 4, 8, 128])
        Vb = sb("Vb", [P, 8, 2, 4, 4, 16])
        mx = sb("mx", [P, 4, 16])
        Ex = sb("Ex", [P, 4, 1024])
        ET = sb("ET", [P, 4, 8, 128])
        mxs = sb("mxs", [P, 4, 16])
        sm = sb("sm", [P, 4, 16])
        rd = sb("rd", [P, 4, 128])
        ri = sb("ri", [P, 4, 16])
        rT = sb("rT", [P, 4, 128])
        bvw = sb("bvw", [P, 128])
        aT = sb("aT", [P, 4, 128])
        hT = sb("hT", [P, 2, E, 128])
        sc = sb("sc", [P, 2, 8])
        top = sb("top", [P, 2, 8])
        tix = sb("tix", [P, 2, 8], U32)
        tif = sb("tif", [P, 2, 2])
        wa = sb("wa", [P, 2, 8])
        wb = sb("wb", [P, 2, 8])
        we = sb("we", [P, 2, 8])
        wep = sb("wep", [P, 2, PIECES], BF16)
        wer = sb("wer", [P, 2, 8])
        weT = sb("weT", [PIECES, 2, 128], BF16)
        acc = sb("acc", [P, 2, 2, 128])
        TG = sb("TG", [P, 2, 128])
        CG = sb("CG", [P, 3, 128])
        AB = sb("AB", [P, 2, 128])
        cU = sb("cU", [P, 128])

        banks = [ctx.enter_context(nc.psum_tensor(f"ps{i}", [P, 512], F32)) for i in range(8)]
        lstm = banks[7]
        ring = [[] for _ in range(7)]
        turn = [0]

        def bank():
            i = turn[0] % 7
            turn[0] += 1
            assert ring[i] is not None, "the reader of this bank has no place yet"
            pe.need(*ring[i])
            ring[i] = None
            return i, banks[i]

        def free(i, mark):
            ring[i] = [mark]

        x_v = a["x"].rearrange("a b d -> (a b) d").rearrange("(t p) d -> p t d", p=P)
        c_v = a["ctx_1024"].rearrange("a b d -> (a b) d").rearrange("(t p) d -> p t d", p=P)
        o_v = out.rearrange("a b d -> (a b) d").rearrange("(t p) d -> p t d", p=P)
        x_in, c_in = {}, {}
        starts = np.cumsum([0] + LOADS)

        def load(q, name, fn):
            s = sem("l_" + name)
            q.dma(fn, s)
            return (s, 16)

        def load_x(c):
            t0, t1 = int(starts[c]), int(starts[c + 1])
            m = load(sp, f"x{c}", lambda e: e.dma_start(x[:, t0:t1, :], x_v[:, t0:t1, :]))
            for t in range(t0, t1):
                x_in[t] = m

        def load_c(c):
            t0, t1 = int(starts[c]), int(starts[c + 1])
            m = load(sp, f"c{c}", lambda e: e.dma_start(cx[:, t0:t1, :], c_v[:, t0:t1, :]))
            for t in range(t0, t1):
                c_in[t] = m

        def column(ap):
            return ap.rearrange("(n a) -> n a", a=1)

        def row(ap):
            return ap.rearrange("(a n) -> a n", a=1)

        W = {}
        in_const = load(act, "const", lambda e: e.dma_start(cst[:, :], const))
        load_x(0)
        load_c(0)
        squares = ["L0_xattn_Wq", "L0_xattn_Wk", "L0_xattn_Wv", "L0_xattn_Wo", "L1_xattn_Wd",
                   "L1_ffn_wf", "L1_ffn_wi", "L1_ffn_wc", "L1_ffn_uf", "L1_ffn_ui", "L1_ffn_uc",
                   "L1_ffn_wo", "L1_ffn_uo"]
        factor = {"L1_ffn_wf": 0.5, "L1_ffn_wi": 0.5, "L1_ffn_uf": 0.25, "L1_ffn_ui": 0.25,
                  "L1_ffn_uc": 0.5, "L1_ffn_uo": 0.5}

        def square(n):
            return load(act if n < 2 else sp, f"sq{n}", lambda e: e.dma_start(wst[:, n, :], a[squares[n]]))

        in_sq = [square(n) for n in range(4)]
        BQ, BK, BV, B1, BF, BI, BC, CI = 0, 1, 2, 3, 11, 12, 13, 14
        cols = {"L0_xattn_bq": BQ, "L0_xattn_bk": BK, "L0_xattn_bv": BV, "L1_ffn_bf": BF,
                "L1_ffn_bi": BI, "L1_ffn_bc": BC, "L1_ffn_in_c": CI}

        def load_col(q, name):
            c = cols[name]
            return load(q, name, lambda e: e.dma_start(col[:, c:c + 1], column(a[name])))

        in_col = {n: load_col(pool, n) for n in ("L0_xattn_bq", "L0_xattn_bk", "L0_xattn_bv")}
        in_bo0 = load(pool, "bo0", lambda e: e.dma_start(bo0[:, :], row(a["L0_xattn_bo"]).to_broadcast([P, 128])))
        def heads(name, tile):
            return load(sp, name, lambda e: e.dma_start(tile[:, :].rearrange("d (h k) -> d h k", h=H),
                                                        a[name].rearrange("h d k -> d h k")))

        load_x(1)
        load_c(1)
        in_k1 = heads("L1_xattn_Wk", wk1)
        in_v1 = heads("L1_xattn_Wv", wv1)
        for c in range(2, 4):
            load_x(c)
            load_c(c)
        in_wg = load(sp, "wg", lambda e: e.dma_start(wg[:, :], a["L0_ffn_W_gate"]))
        in_bg = load(sp, "bg", lambda e: e.dma_start(bg[:, :], row(a["L0_ffn_b_gate"]).to_broadcast([P, 8])))
        in_w1 = load(sp, "w1", lambda e: e.dma_start(w1[:, :, :], a["L0_ffn_W1"].rearrange("e d h -> d e h")))
        in_b1 = load(sp, "b1", lambda e: e.dma_start(col[:, B1:B1 + E], a["L0_ffn_b1"].rearrange("e h -> h e"),
                                                                 allow_slow_non_contiguous=True))
        in_w2 = load(sp, "w2", lambda e: e.dma_start(w2[:, :, :], a["L0_ffn_W2"].rearrange("e d h -> d e h")))
        in_b2 = sem("l_b2")
        for n in range(9):
            sp.dma(lambda e, n=n: e.dma_start(b2[8 * n:8 * n + 8, :], a["L0_ffn_b2"]), in_b2)
        in_q1 = heads("L1_xattn_Wq", wq1)
        in_sq += [square(n) for n in range(4, 13)]
        for n in ("L1_ffn_bf", "L1_ffn_bi", "L1_ffn_bc", "L1_ffn_in_c"):
            in_col[n] = load_col(sp, n)
        in_bo1 = load(sp, "bo1", lambda e: e.dma_start(bo1[:, :], row(a["L1_ffn_bo"]).to_broadcast([P, 128])))
        for c in range(4, len(LOADS)):
            load_x(c)
            load_c(c)

        half = sb("half", [P, 1])
        half_set = pool.done(lambda e: e.memset(half[:, :], -0.5))
        vb_set = [pool.done(lambda e: e.memset(Vb[:, 0:4, :, :, :, :], 0.0))]

        act.need(in_const)
        identb_set = act.done(lambda e: e.activation(identb[:, :], ident, ACT.Copy))

        w_ready = {}

        def turn_weight(n):
            i, b = bank()
            pe.need(in_const, in_sq[n])
            m = pe.done(lambda e: e.transpose(b[:, 0:128], wst[:, n, :], ident))
            act.need(m)
            f = factor.get(squares[n], 1.0)
            m = act.done(lambda e: e.activation(wT[:, n, :], b[:, 0:128], ACT.Copy, scale=f))
            free(i, m)
            w_ready[n] = m

        WQ, WK, WV, WO, WD, WF, WI, WC, UF, UI, UC, WX, UO = range(13)

        M = {}

        def ctx_turn(t):
            i, b = bank()
            pe.need(in_const, c_in[t])
            m = pe.done(lambda e: e.transpose(b[:, 0:128], cx[:, t, :], ident))
            act.need(m)
            M["cT", t] = act.done(lambda e: e.activation(cx[:, t, :], b[:, 0:128], ACT.Copy))
            free(i, M["cT", t])

        def keys_values(L, t):
            i, b = bank()
            wk, wv = (wT[:, WK, :], wT[:, WV, :]) if L == 0 else (wk1[:, :], wv1[:, :])
            pe.need(M["cT", t])
            pe.need(*((w_ready[WK], w_ready[WV]) if L == 0 else (in_k1, in_v1)))
            pe.op(lambda e: e.matmul(b[:, 0:128], wk, cx[:, t, :], start=True, stop=True))
            wv2 = wv.rearrange("p (n two d) -> p two n d", two=2, d=8)
            for s in range(2):
                for h in range(2):
                    fn = (lambda e, s=s, h=h: e.matmul(b[64 * h:64 * h + 64, 128 + 64 * s:192 + 64 * s],
                                                       cx[:, t, 64 * s:64 * s + 64], wv2[:, h, :, :],
                                                       start=True, stop=True, skip_group_check=True))
                    if (s, h) == (1, 1):
                        kv = pe.done(fn)
                    else:
                        pe.op(fn)
            act.need(kv)
            if L == 1:
                if t >= AHEAD:
                    act.need(M["K", 1, t - AHEAD], M["V", 1, t - AHEAD])
                m = act.done(lambda e: e.activation(kv1[:, t % AHEAD, :], b[:, 0:256], ACT.Copy))
                free(i, m)
                M["kv1", t] = m
                return
            act.need(vb_set[0])
            if t >= 4:
                act.need(M["pv", 0, t - 4])
            for h in range(2):
                src = b[64 * h:64 * h + 64, 128:256].rearrange("p (g two d) -> p g two d", two=2, d=8)
                dst = Vb[64 * h:64 * h + 64, t % 4, :, :, 0:4:3, 8 * h:8 * h + 8].rearrange("p s j w d -> p (s j) w d")
                m = act.done(lambda e, src=src, dst=dst: e.activation(dst, src, ACT.Copy))
            M["V", 0, t] = m
            if t >= 2:
                act.need(M["K", 0, t - 2])
            act.need(in_col["L0_xattn_bk"])
            m = act.done(lambda e: e.activation(kT[:, t % 2, :], b[:, 0:128], ACT.Identity, bias=col[:, BK:BK + 1]))
            free(i, m)
            pool.need(m)
            mask_keys(0, t, kT[:, t % 2, :])

        def mask_keys(L, t, k):
            pool.need(in_const)
            if t >= 2:
                pool.need(M["S", L, t - 2])
            M["K", L, t] = pool.done(lambda e: e.tensor_tensor(
                Km[:, 2 * L + t % 2, :, :], k.unsqueeze(1).to_broadcast([P, 8, 128]),
                hmask.unsqueeze(2).to_broadcast([P, 8, 128]), ALU.mult))

        def spread_keys(t):
            pool.need(M["kv1", t])
            mask_keys(1, t, kv1[:, t % AHEAD, 0:128])

        def spread_values(t):
            n = t % AHEAD
            pool.need(M["kv1", t], vb_set[1], in_const)
            if t >= 4:
                pool.need(M["pv", 1, t - 4])
            for w in range(2):
                src = kv1[:, n, 128:256].rearrange("p (g two d) -> p g two d", two=2, d=8)[:, :, w, :]
                dst = Vb[:, 4 + t % 4, :, :, 3 * w, :].rearrange("p s j (h d) -> p (s j) h d", h=2)
                m = pool.done(lambda e, src=src, dst=dst: e.tensor_tensor(
                    dst, src.unsqueeze(2).to_broadcast([P, 8, 2, 8]),
                    side.unsqueeze(1).unsqueeze(3).to_broadcast([P, 8, 2, 8]), ALU.mult))
            M["V", 1, t] = m

        def stats(k, t):
            s = 2 * k + t % 2
            dve.need((x_in[t], M.get(("x_attn", 0, t)), M.get(("x_moe", t)), M.get(("x_attn", 1, t)))[k])
            if t >= 2:
                dve.need(M["mv", k, t - 2])
            M["st", k, t] = dve.done(lambda e: e.bn_stats(st[:, s, :], x[:, t, :]))

        def spread(k, t):
            s = 2 * k + t % 2
            dve.need(M["st", k, t])
            if t >= 2:
                dve.need(M["n", k, t - 2])
            M["mv", k, t] = m = dve.done(lambda e: e.bn_aggr(mv[:, s, :], st[:, s, :]))
            dve.need(m)
            if t >= 2:
                dve.need(M["rs", k, t - 2])
            m = dve.done(lambda e: e.tensor_scalar(ve[:, s, :], mv[:, s, 1:2], EPS, None, ALU.add))
            pool.need(m, half_set)
            if t >= 2:
                pool.need(M["n", k, t - 2])
            M["rs", k, t] = pool.done(lambda e: e.tensor_tensor(rs[:, s, :], ve[:, s, :], half[:, :], ALU.pow))

        def scale(k, t):
            s = 2 * k + t % 2
            q = pool if k in ON_POOL else dve
            q.need(M["rs", k, t], M["mv", k, t])
            if t >= 2:
                q.need(M["xn_read", k, t - 2])
            M["n", k, t] = q.done(lambda e: e.tensor_scalar(xn[:, s, :], x[:, t, :], mv[:, s, 0:1], rs[:, s, :],
                                                            ALU.subtract, ALU.mult))

        def add_bias(t):
            pool.need(bo0_ready[0], M["n", 0, t])
            M["xb", t] = pool.done(lambda e: e.tensor_tensor(x[:, t, :], x[:, t, :], bo0[:, :], ALU.add))

        def turn_x(t, k):
            s = 2 * k + t % 2
            i, b = bank()
            pe.need(M["n", k, t])
            m = pe.done(lambda e: e.transpose(b[:, 0:128], xn[:, s, :], ident))
            M["xn_read", k, t] = m
            act.need(m)
            if t >= 2:
                act.need(M["xT_read", k, t - 2])
            m = act.done(lambda e: e.activation(xT[:, s, :], b[:, 0:128], ACT.Copy))
            free(i, m)
            M["xT", k, t] = m

        def query(L, t):
            s = t % 2
            i, b = bank()
            pe.need(M["xT", 2 * L, t])
            pe.need(w_ready[WQ] if L == 0 else in_q1)
            w = wT[:, WQ, :] if L == 0 else wq1[:, :]
            m = pe.done(lambda e: e.matmul(b[:, 0:128], w, xT[:, 4 * L + s, :], start=True, stop=True))
            M["xT_read", 2 * L, t] = m
            act.need(m)
            if t >= 2:
                act.need(M["S", L, t - 2])
            if L == 0:
                act.need(in_col["L0_xattn_bq"])
                m = act.done(lambda e: e.activation(qT[:, s, :], b[:, 0:128], ACT.Identity,
                                                    bias=col[:, BQ:BQ + 1]))
            else:
                m = act.done(lambda e: e.activation(qT[:, 2 + s, :], b[:, 0:128], ACT.Copy))
            free(i, m)
            M["q", L, t] = m

        def scores(L, t):
            s = 2 * L + t % 2
            pe.need(M["q", L, t], M["K", L, t])
            (i0, b0), (i1, b1) = bank(), bank()
            marks = []
            for r, b in ((0, b0), (1, b1)):
                for n in range(2):
                    fn = (lambda e, r=r, b=b, n=n: e.matmul(
                        b[64 * n:64 * n + 64, :].rearrange("p (j k) -> p j k", j=8),
                        qT[64 * r:64 * r + 64, s, 64 * n:64 * n + 64],
                        Km[64 * r:64 * r + 64, s, :, 64 * n:64 * n + 64],
                        start=True, stop=True, skip_group_check=True))
                    if n:
                        marks.append(pe.done(fn))
                    else:
                        pe.op(fn)
            M["S", L, t] = marks[1]
            M["S_in", L, t] = ((i0, b0, marks[0]), (i1, b1, marks[1]))

        def differences(L, r, t):
            s = 2 * L + t % 2
            i, b, scored = M["S_in", L, t][r]
            S = b[:, :].rearrange("p (j k) -> p j k", j=8)
            mr = mx[:, s, 8 * r:8 * r + 8]
            Er = Ex[:, s, 512 * r:512 * r + 512]
            dve.need(scored)
            m = dve.done(lambda e: e.tensor_reduce(mr, S, AX.X, ALU.max))
            dve.need(m)
            if (L, r) in DIRECT:
                nr = mxs[:, s, 8 * r:8 * r + 8]
                if t >= 2:
                    dve.need(M["E", r, L, t - 2])
                M["D", r, L, t] = dve.done(lambda e: e.tensor_scalar(nr, mr, -SCALE, None, ALU.mult))
                return
            if t >= 2:
                dve.need(M["ET_mm", r, L, t - 2])
            M["D", r, L, t] = dve.done(lambda e: e.tensor_tensor(
                Er.rearrange("p (j k) -> p j k", j=8), S,
                mr.unsqueeze(2).to_broadcast([P, 8, 64]), ALU.subtract))
            free(i, M["D", r, L, t])

        def exps(L, r, t):
            s = 2 * L + t % 2
            Er = Ex[:, s, 512 * r:512 * r + 512]
            act.need(M["D", r, L, t])
            if (L, r) not in DIRECT:
                M["E", r, L, t] = act.done(lambda e: e.activation(Er, Er, ACT.Exp, scale=SCALE))
                return
            i, b, scored = M["S_in", L, t][r]
            if t >= 2:
                act.need(M["ET_mm", r, L, t - 2], M["ri", L, t - 2])
            for j in range(8):
                n = 8 * r + j
                m = act.done(lambda e, j=j, n=n: e.activation(
                    Er[:, 64 * j:64 * j + 64], b[:, 64 * j:64 * j + 64], ACT.Exp, scale=SCALE,
                    bias=mxs[:, s, n:n + 1], accum_out=sm[:, s, n:n + 1]))
            M["E", r, L, t] = M["sm", r, L, t] = m
            free(i, m)

        def sums(L, r, t):
            if (L, r) in DIRECT:
                return
            s = 2 * L + t % 2
            dve.need(M["E", r, L, t])
            M["sm", r, L, t] = dve.done(lambda e: e.tensor_reduce(
                sm[:, s, 8 * r:8 * r + 8], Ex[:, s, 512 * r:512 * r + 512].rearrange("p (j k) -> p j k", j=8),
                AX.X, ALU.add))

        def inverse(L, t):
            s = 2 * L + t % 2
            dve.need(M["sm", 0, L, t], M["sm", 1, L, t])
            if t >= 2:
                dve.need(M["rd", L, t - 2])
            M["ri", L, t] = dve.done(lambda e: e.reciprocal(ri[:, s, :], sm[:, s, :]))

        def widen(L, t):
            s = 2 * L + t % 2
            act.need(M["ri", L, t])
            if t >= 2:
                act.need(M["rd_mm", L, t - 2])
            M["rd", L, t] = act.done(lambda e: e.activation(
                rd[:, s, :].rearrange("p (h d) -> p h d", d=8),
                ri[:, s, :].unsqueeze(2).to_broadcast([P, 16, 8]), ACT.Copy))

        def turn_r(L, t):
            s = 2 * L + t % 2
            i, b = bank()
            pe.need(M["rd", L, t])
            M["rd_mm", L, t] = m = pe.done(lambda e: e.transpose(b[:, 0:128], rd[:, s, :], ident))
            act.need(m)
            if t >= 2:
                act.need(M["aT", L, t - 2])
            M["rT", L, t] = act.done(lambda e: e.activation(rT[:, s, :], b[:, 0:128], ACT.Copy))
            free(i, M["rT", L, t])

        def turn_e(L, r, t):
            s = 2 * L + t % 2
            i, b = bank()
            pe.need(M["E", r, L, t])
            for n in range(4):
                g = 4 * r + n
                fn = (lambda e, n=n, g=g: e.transpose(b[:, 128 * n:128 * n + 128],
                                                      Ex[:, s, 128 * g:128 * g + 128], ident))
                if n == 3:
                    m = pe.done(fn)
                else:
                    pe.op(fn)
            M["ET_mm", r, L, t] = m
            act.need(m)
            if t >= 2:
                act.need(M["pv", L, t - 2])
            M["ET", r, L, t] = act.done(lambda e: e.activation(
                ET[:, s, 4 * r:4 * r + 4, :], b[:, :].rearrange("p (n q) -> p n q", n=4), ACT.Copy))
            free(i, M["ET", r, L, t])

        def values(L, t):
            s = 2 * L + t % 2
            vs = 4 * L + t % 4
            i, b = bank()
            pe.need(M["ET", 0, L, t], M["ET", 1, L, t], M["V", L, t])
            for n in range(2):
                for w in range(2):
                    for j in range(4):
                        fn = (lambda e, n=n, w=w, j=j: e.matmul(
                            b[32 * j:32 * j + 32, 64 * n:64 * n + 64],
                            Vb[:, vs, n, j, 2 * w:2 * w + 2, :].rearrange("p a c -> p (a c)"),
                            ET[:, s, 2 * j + w, 64 * n:64 * n + 64],
                            start=(w == 0), stop=(w == 1), skip_group_check=True))
                        if (n, w, j) == (1, 1, 3):
                            m = pe.done(fn)
                        else:
                            pe.op(fn)
            M["pv", L, t] = m
            M["pv_in", L, t] = (i, b, m)

        def normal(L, t):
            s = 2 * L + t % 2
            i, b, m = M["pv_in", L, t]
            dve.need(m, M["rT", L, t])
            if t >= 2:
                dve.need(M["o_mm", L, t - 2])
            M["aT", L, t] = dve.done(lambda e: e.tensor_tensor(aT[:, s, :], b[:, 0:128], rT[:, s, :], ALU.mult))
            free(i, M["aT", L, t])

        def project(L, t):
            s = 2 * L + t % 2
            n = WO if L == 0 else WD
            i, b = bank()
            pe.need(M["aT", L, t], w_ready[n])
            m = pe.done(lambda e: e.matmul(b[:, 0:128], aT[:, s, :], wT[:, n, :], start=True, stop=True))
            M["o_mm", L, t] = m
            dve.need(m)
            if L == 0:
                dve.need(M["xb", t])
            m = dve.done(lambda e: e.tensor_tensor(x[:, t, :], b[:, 0:128], x[:, t, :], ALU.add))
            free(i, m)
            M["x_attn", L, t] = m

        def gate(t):
            s = t % 2
            i, b = bank()
            pe.need(M["xT", 1, t], in_wg)
            m = pe.done(lambda e: e.matmul(b[:, 0:8], xT[:, 2 + s, :], wg[:, :], start=True, stop=True))
            dve.need(m, in_bg)
            m = dve.done(lambda e: e.tensor_tensor(sc[:, s, :], b[:, 0:8], bg[:, :], ALU.add))
            free(i, m)
            M["sc", t] = m

        def gate_top(t):
            s = t % 2
            dve.need(M["sc", t])
            m = dve.done(lambda e: e.max(top[:, s, :], sc[:, s, :]))
            dve.need(m)
            m = dve.done(lambda e: e.max_index(tix[:, s, :], top[:, s, :], sc[:, s, :]))
            M["tix", t] = m

        def gate_index(t):
            s = t % 2
            dve.need(M["tix", t])
            M["tif", t] = dve.done(lambda e: e.tensor_copy(tif[:, s, :], tix[:, s, 0:2]))

        def gate_weights(t):
            s = t % 2
            dve.need(M["tif", t], in_const)
            m = dve.done(lambda e: e.tensor_scalar(wa[:, s, :], iota, tif[:, s, 0:1], top[:, s, 0:1],
                                                   ALU.is_equal, ALU.mult))
            m = dve.done(lambda e: e.tensor_scalar(wb[:, s, :], iota, tif[:, s, 1:2], top[:, s, 1:2],
                                                   ALU.is_equal, ALU.mult))
            dve.need(m)
            if t >= 2:
                dve.need(M["wep", t - 2])
            M["we", t] = dve.done(lambda e: e.tensor_tensor(we[:, s, :], wa[:, s, :], wb[:, s, :], ALU.add))

        def gate_pieces(t):
            s = t % 2

            def out(n):
                return wep[:, s, 24 * n:24 * n + 24].rearrange("p (j k) -> p j k", j=3)

            def wide(v):
                return v.unsqueeze(1).to_broadcast([P, 3, 8])

            pool.need(M["we", t])
            if t >= 2:
                pool.need(M["we_mm", t - 2])
            m = pool.done(lambda e: e.tensor_copy(out(0), wide(we[:, s, :])))
            pool.need(m)
            m = pool.done(lambda e: e.tensor_tensor(wer[:, s, :], we[:, s, :], wep[:, s, 0:8], ALU.subtract))
            pool.need(m)
            m = pool.done(lambda e: e.tensor_copy(out(1), wide(wer[:, s, :])))
            pool.need(m)
            M["wep", t] = pool.done(lambda e: e.tensor_tensor(out(2), wide(wer[:, s, :]),
                                                              wide(wep[:, s, 24:32]), ALU.subtract))

        def hidden(c, t):
            s = t % 2
            pe.need(M["xT", 1, t], in_w1)
            i, b = bank()
            for n in range(4):
                fn = (lambda e, n=n: e.matmul(b[:, 128 * n:128 * n + 128], w1[:, 4 * c + n, :], xT[:, 2 + s, :],
                                              start=True, stop=True, skip_group_check=True))
                if n == 3:
                    m = pe.done(fn)
                else:
                    pe.op(fn)
            M["h_in", c, t] = (i, b, m)
            M["xT_read", 1, t] = m

        def relus(c, t):
            s = t % 2
            i, b, m = M["h_in", c, t]
            act.need(m, in_b1)
            if t >= 2:
                act.need(M["y_mm", c, t - 2])
            for n in range(4):
                k = 4 * c + n
                fn = (lambda e, n=n, k=k: e.activation(hT[:, s, k, :], b[:, 128 * n:128 * n + 128],
                                                       ACT.Relu, bias=col[:, B1 + k:B1 + k + 1]))
                if n == 3:
                    M["h", c, t] = act.done(fn)
                else:
                    act.op(fn)
            free(i, M["h", c, t])

        def turn_w(t):
            s = t % 2
            i, b = bank()
            pe.need(M["wep", t], identb_set)
            m = pe.done(lambda e: e.matmul(b[0:PIECES, 0:128], wep[:, s, :], identb[:, :], start=True, stop=True))
            M["we_mm", t] = m
            act.need(m)
            if t >= 2:
                act.need(M["b2_mm", t - 2])
            M["weT", t] = act.done(lambda e: e.activation(weT[:, s, :], b[0:PIECES, 0:128], ACT.Copy))
            free(i, M["weT", t])

        def experts(c, t):
            s = t % 2
            i, b = bank()
            pe.need(M["h", c, t], in_w2)
            for n in range(4):
                k = 4 * c + n
                fn = (lambda e, k=k, n=n: e.matmul(b[:, 128 * n:128 * n + 128], hT[:, s, k, :], w2[:, k, :],
                                                   start=True, stop=True, skip_group_check=True))
                if n == 3:
                    m = pe.done(fn)
                else:
                    pe.op(fn)
            M["y_mm", c, t] = m
            M["y_in", c, t] = (i, b, m)

        def expert_bias(t):
            s = t % 2
            i, b = bank()
            pe.need(M["weT", t], M["b2s"])
            m = pe.done(lambda e: e.matmul(b[:, 0:128], weT[:, s, :], b2s[:, :], start=True, stop=True))
            M["b2_mm", t] = m
            act.need(m)
            if t >= 2:
                act.need(M["acc_read", t - 2])
            M["eb", t] = act.done(lambda e: e.activation(acc[:, s, 1, :], b[:, 0:128], ACT.Copy))
            free(i, M["eb", t])

        def combine(h, t):
            s = t % 2
            if h == 0 and t >= 2:
                dve.need(M["acc_read", t - 2])
            dve.need(M["we", t])
            for n in (2 * h, 2 * h + 1):
                for c in range(2):
                    i, b, m = M["y_in", c, t]
                    dve.need(m)
                    k = 4 * c + n
                    y = b[:, 128 * n:128 * n + 128]
                    w = we[:, s, k:k + 1]
                    d = acc[:, s, c, :]
                    if n == 0 and c == 0:
                        src = x[:, t, :]
                    elif n == 0:
                        dve.need(M["eb", t])
                        src = d
                    else:
                        dve.need(M["acc", c, t])
                        src = d
                    M["acc", c, t] = dve.done(lambda e, y=y, w=w, d=d, src=src: e.scalar_tensor_tensor(
                        d, y, w, src, ALU.mult, ALU.add))
                    if n == 3:
                        free(i, M["acc", c, t])
            if h == 1:
                q = pool if SUM_ON_POOL else dve
                q.need(M["acc", 0, t], M["acc", 1, t])
                m = q.done(lambda e: e.tensor_tensor(x[:, t, :], acc[:, s, 0, :], acc[:, s, 1, :], ALU.add))
                M["x_moe", t] = M["acc_read", t] = m

        def inputs(t):
            s = t % 2
            i, b = bank()
            pe.need(M["xT", 3, t], w_ready[WX], w_ready[WF], w_ready[WI], w_ready[WC])
            m = pe.done(lambda e: e.matmul(b[:, 0:128], xT[:, 6 + s, :], wT[:, WX, :], start=True, stop=True))
            act.need(m)
            act.need(M["kv1", t])
            M["xo", t] = act.done(lambda e: e.activation(cx[:, t, :], b[:, 0:128], ACT.Copy))
            free(i, M["xo", t])
            if t:
                pe.need(M["gates", 2 * t - 1])
            for n, w in enumerate((WF, WI, WC)):
                fn = (lambda e, n=n, w=w: e.matmul(lstm[:, 128 * n:128 * n + 128], wT[:, w, :], xT[:, 6 + s, :],
                                                   start=(n == 0), stop=False, skip_group_check=True))
                if n == 2:
                    M["xT_read", 3, t] = pe.done(fn)
                else:
                    pe.op(fn)

        def step(k):
            t, o = k // 2, 64 * (k % 2)
            assert ("xT_read", 3, t) in M, "the cell's products with its input come first"
            pe.need(M["C", k - 1], w_ready[UF], w_ready[UI], w_ready[UC])
            c_in_now = CG[:, k % 3, 0:64]
            for n, w in enumerate((UF, UI, UC)):
                fn = (lambda e, n=n, w=w: e.matmul(lstm[:, 128 * n + o:128 * n + o + 64], wT[:, w, :], c_in_now,
                                                   start=False, stop=True, skip_group_check=True))
                if n == 2:
                    m = pe.done(fn)
                else:
                    pe.op(fn)
            M["z", k] = m

        def gates(k):
            o = 64 * (k % 2)
            act.need(M["z", k])
            if k >= 2:
                act.need(M["AB", k - 2])
            act.need(cols_half, in_col["L1_ffn_bc"])
            act.op(lambda e: e.activation(TG[:, k % 2, 0:64], lstm[:, o:o + 64], ACT.Tanh, bias=col[:, BF + 4:BF + 5]))
            act.op(lambda e: e.activation(TG[:, k % 2, 64:128], lstm[:, 128 + o:192 + o], ACT.Tanh,
                                          bias=col[:, BF + 5:BF + 6]))
            M["gates", k] = act.done(lambda e: e.activation(CG[:, k % 3, 64:128], lstm[:, 256 + o:320 + o],
                                                            ACT.Tanh, bias=col[:, BC:BC + 1]))

        def update(k):
            dve.need(M["gates", k], M["C", k - 1])
            M["AB", k] = dve.done(lambda e: e.scalar_tensor_tensor(AB[:, k % 2, :], TG[:, k % 2, :], 1.0,
                                                                   CG[:, k % 3, :], ALU.add, ALU.mult))
            dve.need(M["AB", k])
            M["C", k] = dve.done(lambda e: e.scalar_tensor_tensor(CG[:, (k + 1) % 3, 0:64], AB[:, k % 2, 0:64], 0.5,
                                                                  AB[:, k % 2, 64:128], ALU.mult, ALU.add))

        for n in (WQ, WK, WV, WO):
            turn_weight(n)

        stages = {
            "stepA": lambda t: step(2 * t),
            "gA": lambda t: gates(2 * t),
            "ctx": lambda t: ctx_turn(t),
            "st0": lambda t: stats(0, t),
            "st1": lambda t: stats(1, t),
            "st2": lambda t: stats(2, t),
            "st3": lambda t: stats(3, t),
            "sp0": lambda t: spread(0, t),
            "sp1": lambda t: spread(1, t),
            "sp2": lambda t: spread(2, t),
            "sp3": lambda t: spread(3, t),
            "scale0": lambda t: scale(0, t),
            "kv0": lambda t: keys_values(0, t),
            "turnx0": lambda t: turn_x(t, 0),
            "xb": lambda t: add_bias(t),
            "q0": lambda t: query(0, t),
            "turnw": lambda t: turn_w(t),
            "y0": lambda t: experts(0, t),
            "y1": lambda t: experts(1, t),
            "c0": lambda t: combine(0, t),
            "c1": lambda t: combine(1, t),
            "yb": lambda t: expert_bias(t),
            "updA": lambda t: update(2 * t),
            "S0": lambda t: scores(0, t),
            "d00": lambda t: differences(0, 0, t),
            "d01": lambda t: differences(0, 1, t),
            "S1": lambda t: scores(1, t),
            "d10": lambda t: differences(1, 0, t),
            "d11": lambda t: differences(1, 1, t),
            "x00": lambda t: exps(0, 0, t),
            "x01": lambda t: exps(0, 1, t),
            "x10": lambda t: exps(1, 0, t),
            "x11": lambda t: exps(1, 1, t),
            "e00": lambda t: turn_e(0, 0, t),
            "e01": lambda t: turn_e(0, 1, t),
            "e10": lambda t: turn_e(1, 0, t),
            "e11": lambda t: turn_e(1, 1, t),
            "v0": lambda t: values(0, t),
            "v1": lambda t: values(1, t),
            "gate": lambda t: gate(t),
            "gtop": lambda t: gate_top(t),
            "gidx": lambda t: gate_index(t),
            "gw": lambda t: gate_weights(t),
            "gp": lambda t: gate_pieces(t),
            "km1": lambda t: spread_keys(t),
            "vm1": lambda t: spread_values(t),
            "h0": lambda t: hidden(0, t),
            "h1": lambda t: hidden(1, t),
            "r0": lambda t: relus(0, t),
            "r1": lambda t: relus(1, t),
            "s00": lambda t: sums(0, 0, t),
            "s01": lambda t: sums(0, 1, t),
            "i0": lambda t: inverse(0, t),
            "w0": lambda t: widen(0, t),
            "n0": lambda t: normal(0, t),
            "rt0": lambda t: turn_r(0, t),
            "s10": lambda t: sums(1, 0, t),
            "s11": lambda t: sums(1, 1, t),
            "i1": lambda t: inverse(1, t),
            "w1": lambda t: widen(1, t),
            "n1": lambda t: normal(1, t),
            "rt1": lambda t: turn_r(1, t),
            "p0": lambda t: project(0, t),
            "p1": lambda t: project(1, t),
            "stepB": lambda t: step(2 * t + 1),
            "gB": lambda t: gates(2 * t + 1),
            "turnx1": lambda t: turn_x(t, 1),
            "turnx2": lambda t: turn_x(t, 2),
            "turnx3": lambda t: turn_x(t, 3),
            "kv1": lambda t: keys_values(1, t),
            "q1": lambda t: query(1, t),
            "inputs": lambda t: inputs(t),
            "scale1": lambda t: scale(1, t),
            "scale2": lambda t: scale(2, t),
            "scale3": lambda t: scale(3, t),
            "updB": lambda t: update(2 * t + 1),
        }

        cols_half = None

        def recurrent_setup():
            act.need(in_col["L1_ffn_bf"], in_col["L1_ffn_bi"], in_col["L1_ffn_in_c"])
            m = act.done(lambda e: e.activation(col[:, BF + 4:BF + 6], col[:, BF:BF + 2], ACT.Copy, scale=0.5))
            M["C", -1] = act.done(lambda e: e.activation(CG[:, 0, 0:64], col[:, CI:CI + 1].to_broadcast([P, 64]),
                                                         ACT.Copy, scale=2.0))
            return m

        bo0_ready = []

        def project_bias():
            act.need(in_col["L0_xattn_bv"])
            m = act.done(lambda e: e.activation(bvw[:, :], col[:, BV:BV + 1].to_broadcast([P, 128]), ACT.Copy))
            i, b = bank()
            pe.need(m, w_ready[WO])
            m = pe.done(lambda e, b=b: e.matmul(b[:, 0:128], bvw[:, :], wT[:, WO, :], start=True, stop=True))
            dve.need(m, in_bo0)
            bo0_set = dve.done(lambda e, b=b: e.tensor_tensor(bo0[:, :], b[:, 0:128], bo0[:, :], ALU.add))
            free(i, bo0_set)
            bo0_ready.append(bo0_set)

        def clear_values():
            vb_set.append(pool.done(lambda e: e.memset(Vb[:, 4:8, :, :, :, :], 0.0)))

        def bias_pieces():
            dve.need((in_b2, 144), in_const)
            for n in range(3):
                m = dve.done(lambda e, n=n: e.tensor_copy(b2p[:, n, :], b2[:, :]))
                dve.need(m)
                if n < 2:
                    m = dve.done(lambda e, n=n: e.tensor_tensor(b2[:, :], b2[:, :], b2p[:, n, :], ALU.subtract))
                    dve.need(m)
            m = dve.done(lambda e: e.tensor_scalar(b2s[:, :], b2p[:, 0, :], piece[0:PIECES, 0:1], None, ALU.mult))
            for n in (1, 2):
                dve.need(m)
                m = dve.done(lambda e, n=n: e.scalar_tensor_tensor(
                    b2s[:, :], b2p[:, n, :], piece[0:PIECES, n:n + 1], b2s[:, :], ALU.mult, ALU.add))
            M["b2s"] = m

        turns = sorted((t + p, n, t) for n, p in PLACE.items() for t in range(NT))
        setup = [project_bias] + [lambda n=n: turn_weight(n) for n in range(4, 13)] + [recurrent_setup, bias_pieces, clear_values]
        for at, n, t in turns:
            while setup and at >= SETUP + 0.15 * (13 - len(setup)):
                m = setup.pop(0)()
                cols_half = m or cols_half
            stages[n](t)

        i, b = bank()
        K = 2 * NT - 1
        pe.need(M["C", K], w_ready[UO])
        pe.op(lambda e: e.matmul(b[0:64, 0:128], CG[:, (K + 1) % 3, 0:64], wT[:, UO, :], start=True, stop=True))
        m = pe.done(lambda e: e.matmul(b[64:128, 0:128], CG[:, (K + 1) % 3, 0:64], wT[:, UO, :],
                                       start=True, stop=True, skip_group_check=True))
        dve.need(m, in_bo1)
        cu = dve.done(lambda e: e.tensor_tensor(cU[:, :], b[:, 0:128], bo1[:, :], ALU.add))
        s_out = sem("s_out")
        n_out = 0
        waiting = {dve: [], pool: []}
        lo = 0

        def finish(adder):
            ts, m = waiting[adder].pop(0)
            adder.need(m, M["x_attn", 1, NT - 1])
            m = adder.done(lambda e: e.tensor_tensor(x[:, ts, :], cx[:, ts, :], x[:, ts, :], ALU.add))
            sp.need(m)
            sp.dma(lambda e: e.dma_start(o_v[:, ts, :], x[:, ts, :]), s_out)

        for adder, n in TAIL:
            ts, n_out, lo = slice(lo, lo + n), n_out + 16, lo + n
            q = dve if adder == "dve" else pool
            q.need(cu, M["xo", NT - 1])
            m = q.done(lambda e, ts=ts, n=n: e.tensor_tensor(
                cx[:, ts, :], cx[:, ts, :], cU[:, :].unsqueeze(1).to_broadcast([P, n, 128]), ALU.add))
            act.need(m)
            m = act.done(lambda e, ts=ts: e.activation(cx[:, ts, :], cx[:, ts, :], ACT.Tanh))
            waiting[q].append((ts, m))
            if len(waiting[q]) > DEPTH:
                finish(q)
        for _ in range(DEPTH):
            for q in (dve, pool):
                if waiting[q]:
                    finish(q)
        sp.need((s_out, n_out))

        block = ctx.enter_context(nc.Block())

        @block.tensor
        def _(e):
            pe.run(e)

        @block.vector
        def _(e):
            dve.run(e)

        @block.scalar
        def _(e):
            act.run(e)

        @block.gpsimd
        def _(e):
            pool.run(e)

        @block.sync
        def _(e):
            sp.run(e)


_INS = ["x", "ctx_1024", "L0_xattn_Wq", "L0_xattn_bq", "L0_xattn_Wk", "L0_xattn_bk", "L0_xattn_Wv", "L0_xattn_bv",
        "L0_xattn_Wo", "L0_xattn_bo", "L0_ffn_W_gate", "L0_ffn_b_gate", "L0_ffn_W1", "L0_ffn_b1", "L0_ffn_W2",
        "L0_ffn_b2", "L1_xattn_Wq", "L1_xattn_Wk", "L1_xattn_Wv", "L1_xattn_Wd", "L1_ffn_wf", "L1_ffn_uf",
        "L1_ffn_bf", "L1_ffn_wi", "L1_ffn_ui", "L1_ffn_bi", "L1_ffn_wc", "L1_ffn_uc", "L1_ffn_bc", "L1_ffn_wo",
        "L1_ffn_uo", "L1_ffn_bo", "L1_ffn_in_c"]


def constants():
    c = np.zeros((P, 149), np.float32)
    c[:, 0:128] = np.eye(128, dtype=np.float32)
    p = np.arange(P)
    c[p, 128 + (p % 64) // 8] = 1.0
    c[:, 136:144] = np.arange(8, dtype=np.float32)
    c[p, 147 + p // 64] = 1.0
    for m in range(3):
        c[p, 144 + m] = (p // 8) % 3 == m
    return c


def kernel(**inputs):
    import numpy as _np
    import concourse.bacc as _bacc
    from concourse import mybir as _mybir
    from concourse.bass_utils import run_bass_kernel_spmd as _run

    nc = _bacc.Bacc("TRN2", target_bir_lowering=False, num_devices=1)
    arrays, aps = {}, {}
    for name in _INS:
        v = _np.ascontiguousarray(inputs[name])
        arrays[f"in_{name}_dram"] = v
        aps[name] = nc.dram_tensor(f"in_{name}_dram", v.shape, _mybir.dt.from_np(v.dtype), kind="ExternalInput").ap()
    c = constants()
    arrays["constants_dram"] = c
    cap = nc.dram_tensor("constants_dram", c.shape, F32, kind="ExternalInput").ap()
    out = nc.dram_tensor("out_0_dram", (128, 64, 128), F32, kind="ExternalOutput").ap()
    build(nc, aps, cap, out)
    r = _run(nc, [arrays], core_ids=[0])
    return r.results[0]["out_0_dram"]
```
